# Optimizing a Trainium2 kernel written in Bass

```python
import numpy as np
import jax
import jax.numpy as jnp

def _softmax(x, axis=-1):
    return jax.nn.softmax(x, axis=axis)

def _gelu(x):
    return jax.nn.gelu(x, approximate=True)

def _silu(x):
    return jax.nn.silu(x)

def _sigmoid(x):
    return jax.nn.sigmoid(x)

def _layernorm(x, axis=-1, eps=1e-05):
    m = jnp.mean(x, axis=axis, keepdims=True)
    v = jnp.var(x, axis=axis, keepdims=True)
    return (x - m) / jnp.sqrt(v + eps)

def _scatter_add(tgt, idx, src, axis=0):
    return tgt.at[idx].add(src)

def _segment_sum(src, seg, n):
    return jax.ops.segment_sum(src, seg, n)
kernel_name = 'mk_adaln_d1_jaxref_r8_ad37ce'

def setup_inputs(seed: int=0):
    np.random.seed(seed)
    _w = jnp.asarray

    def _L0_attn_setup():
        import jax, jax.numpy as jnp
        import numpy as np
        H = 512
        D = 1024
        N = 16
        K = 4
        R = 32
        BATCH = 1
        L = 256
        EPS = 1e-06

        def _rmsnorm(x, w):
            return x * jax.lax.rsqrt(jnp.mean(x * x, axis=-1, keepdims=True) + EPS) * w
        key = jax.random.key(seed)
        ks = jax.random.split(key, 10)
        s = 0.02
        return {'hidden_states': jax.random.normal(ks[0], (BATCH, L, H), jnp.float32), 'W_in': jax.random.normal(ks[1], (2 * D, H), jnp.float32) * s, 'conv_w': jax.random.normal(ks[2], (D, K), jnp.float32) * s, 'conv_b': jax.random.normal(ks[3], (D,), jnp.float32) * s, 'Wx': jax.random.normal(ks[4], (R + 2 * N, D), jnp.float32) * s, 'dt_ln_w': jnp.ones((R,), jnp.float32), 'b_ln_w': jnp.ones((N,), jnp.float32), 'c_ln_w': jnp.ones((N,), jnp.float32), 'Wdt': jax.random.normal(ks[5], (D, R), jnp.float32) * s, 'dt_bias': jax.random.normal(ks[6], (D,), jnp.float32) * s, 'A': -jnp.exp(jax.random.normal(ks[7], (D, N), jnp.float32) * 0.5), 'D_param': jnp.ones((D,), jnp.float32), 'W_out': jax.random.normal(ks[8], (H, D), jnp.float32) * s}
    _L0_attn_in = _L0_attn_setup()

    def _L0_ffn_setup():
        import jax, jax.numpy as jnp
        import numpy as np
        B, S, IN, OUT = (4, 256, 512, 512)
        E, K, R = (8, 2, 16)
        CAP_FACTOR = 3.0
        ALPHA = 1.0 / R
        LN_EPS = 1e-05
        key = jax.random.key(seed)
        ks = jax.random.split(key, 6)
        return {'x': jax.random.normal(ks[0], (B, S, IN), dtype=jnp.float32), 'weight': jax.random.normal(ks[1], (OUT, IN), dtype=jnp.float32) * 0.02, 'lora_A': jax.random.normal(ks[2], (E, IN, R), dtype=jnp.float32) / np.sqrt(R), 'lora_B': jax.random.normal(ks[3], (E, R, OUT), dtype=jnp.float32) * 0.02, 'gw1': jax.random.normal(ks[4], (4 * E, IN), dtype=jnp.float32) * 0.02, 'gb1': jnp.zeros((4 * E,), dtype=jnp.float32), 'ln_gamma': jnp.ones((4 * E,), dtype=jnp.float32), 'ln_beta': jnp.zeros((4 * E,), dtype=jnp.float32), 'gw2': jax.random.normal(ks[5], (E, 4 * E), dtype=jnp.float32) * 0.02, 'gb2': jnp.zeros((E,), dtype=jnp.float32)}
    _L0_ffn_in = _L0_ffn_setup()
    _L0_c = _w((lambda *s: np.random.randn(*s).astype(np.float32) * 0.05)(1, 512))
    _L0_wmod = _w((lambda *s: np.random.randn(*s).astype(np.float32) * 0.05)(512, 6 * 512) * 512 ** (-0.5))
    _d = {'L0_attn_hidden_states': _L0_attn_in['hidden_states'], 'L0_attn_W_in': _L0_attn_in['W_in'], 'L0_attn_conv_w': _L0_attn_in['conv_w'], 'L0_attn_conv_b': _L0_attn_in['conv_b'], 'L0_attn_Wx': _L0_attn_in['Wx'], 'L0_attn_dt_ln_w': _L0_attn_in['dt_ln_w'], 'L0_attn_b_ln_w': _L0_attn_in['b_ln_w'], 'L0_attn_c_ln_w': _L0_attn_in['c_ln_w'], 'L0_attn_Wdt': _L0_attn_in['Wdt'], 'L0_attn_dt_bias': _L0_attn_in['dt_bias'], 'L0_attn_A': _L0_attn_in['A'], 'L0_attn_D_param': _L0_attn_in['D_param'], 'L0_attn_W_out': _L0_attn_in['W_out'], 'L0_ffn_weight': _L0_ffn_in['weight'], 'L0_ffn_lora_A': _L0_ffn_in['lora_A'], 'L0_ffn_lora_B': _L0_ffn_in['lora_B'], 'L0_ffn_gw1': _L0_ffn_in['gw1'], 'L0_ffn_gb1': _L0_ffn_in['gb1'], 'L0_ffn_ln_gamma': _L0_ffn_in['ln_gamma'], 'L0_ffn_ln_beta': _L0_ffn_in['ln_beta'], 'L0_ffn_gw2': _L0_ffn_in['gw2'], 'L0_ffn_gb2': _L0_ffn_in['gb2'], 'L0_c': _L0_c, 'L0_wmod': _L0_wmod}
    _x0 = _d['L0_attn_hidden_states']
    _d['L0_attn_hidden_states'] = jax.random.normal(jax.random.fold_in(jax.random.key(seed), 1), (1, 1024, 512), dtype=_x0.dtype)
    del _x0
    return _d

def reference(L0_attn_hidden_states, L0_attn_W_in, L0_attn_conv_w, L0_attn_conv_b, L0_attn_Wx, L0_attn_dt_ln_w, L0_attn_b_ln_w, L0_attn_c_ln_w, L0_attn_Wdt, L0_attn_dt_bias, L0_attn_A, L0_attn_D_param, L0_attn_W_out, L0_ffn_weight, L0_ffn_lora_A, L0_ffn_lora_B, L0_ffn_gw1, L0_ffn_gb1, L0_ffn_ln_gamma, L0_ffn_ln_beta, L0_ffn_gw2, L0_ffn_gb2, L0_c, L0_wmod):

    def _L0_attn_ref(hidden_states, W_in, conv_w, conv_b, Wx, dt_ln_w, b_ln_w, c_ln_w, Wdt, dt_bias, A, D_param, W_out):
        import jax, jax.numpy as jnp
        import numpy as np
        H = 512
        D = 1024
        N = 16
        K = 4
        R = 32
        BATCH = 1
        L = 256
        EPS = 1e-06

        def _rmsnorm(x, w):
            return x * jax.lax.rsqrt(jnp.mean(x * x, axis=-1, keepdims=True) + EPS) * w
        proj = hidden_states @ W_in.T
        u, gate = jnp.split(proj, 2, axis=-1)
        x = jnp.transpose(u, (0, 2, 1))
        x = jax.lax.conv_general_dilated(x, conv_w[:, None, :], window_strides=(1,), padding=[(K - 1, 0)], dimension_numbers=('NCH', 'OIH', 'NCH'), feature_group_count=D)
        u = jax.nn.silu(jnp.transpose(x, (0, 2, 1)) + conv_b)
        ssm_p = u @ Wx.T
        dt, Bm, Cm = jnp.split(ssm_p, [R, R + N], axis=-1)
        dt = _rmsnorm(dt, dt_ln_w)
        Bm = _rmsnorm(Bm, b_ln_w)
        Cm = _rmsnorm(Cm, c_ln_w)
        delta = jax.nn.softplus(dt @ Wdt.T + dt_bias)

        def step(state, xs):
            d_t, B_t, C_t, u_t = xs
            dA = jnp.exp(d_t[..., None] * A)
            state = dA * state + (d_t * u_t)[..., None] * B_t[:, None, :]
            y_t = jnp.einsum('bdn,bn->bd', state, C_t)
            return (state, y_t)
        init = jnp.zeros((hidden_states.shape[0], D, N), hidden_states.dtype)
        xs = (jnp.swapaxes(delta, 0, 1), jnp.swapaxes(Bm, 0, 1), jnp.swapaxes(Cm, 0, 1), jnp.swapaxes(u, 0, 1))
        _, ys = jax.lax.scan(step, init, xs)
        y = jnp.swapaxes(ys, 0, 1) + u * D_param
        y = y * jax.nn.silu(gate)
        return y @ W_out.T

    def _L0_ffn_ref(x, weight, lora_A, lora_B, gw1, gb1, ln_gamma, ln_beta, gw2, gb2):
        import jax, jax.numpy as jnp
        import numpy as np
        B, S, IN, OUT = (4, 256, 512, 512)
        E, K, R = (8, 2, 16)
        CAP_FACTOR = 3.0
        ALPHA = 1.0 / R
        LN_EPS = 1e-05
        orig_shape = x.shape
        xf = x.reshape(-1, orig_shape[-1])
        N = xf.shape[0]
        capacity = int(CAP_FACTOR * N / E)
        h = xf @ gw1.T + gb1
        mu = jnp.mean(h, axis=-1, keepdims=True)
        var = jnp.mean((h - mu) ** 2, axis=-1, keepdims=True)
        h = (h - mu) * jax.lax.rsqrt(var + LN_EPS) * ln_gamma + ln_beta
        h = jax.nn.relu(h)
        gates = h @ gw2.T + gb2
        top_v, top_i = jax.lax.top_k(gates, K)
        top_g = jax.nn.softmax(top_v, axis=-1)
        onehot = (top_i[..., None] == jnp.arange(E)).astype(xf.dtype)
        counts = onehot.sum(axis=0)
        allowed = (counts <= capacity).astype(xf.dtype)
        w = jnp.einsum('nke,nk,ke->ne', onehot, top_g, allowed)
        main = xf @ weight.T
        tmp = jnp.einsum('ni,eir->enr', xf, lora_A)
        tmp = tmp * w.T[:, :, None]
        lora = jnp.einsum('enr,ero->no', tmp, lora_B) * ALPHA
        out = main + lora
        return out.reshape(*orig_shape[:-1], weight.shape[0])
    x = L0_attn_hidden_states
    mod = (_silu(L0_c) @ L0_wmod).reshape(L0_c.shape[0], 6, 1, -1)
    sa, ca, ga, sb, cb, gb = (mod[:, 0], mod[:, 1], mod[:, 2], mod[:, 3], mod[:, 4], mod[:, 5])
    ga = (2 * (ga >= 0) - 1) * jnp.maximum(jnp.abs(ga), 0.25)
    gb = (2 * (gb >= 0) - 1) * jnp.maximum(jnp.abs(gb), 0.25)
    h = _layernorm(x, axis=-1) * (1 + ca) + sa
    x = x + ga * _L0_attn_ref(h, L0_attn_W_in, L0_attn_conv_w, L0_attn_conv_b, L0_attn_Wx, L0_attn_dt_ln_w, L0_attn_b_ln_w, L0_attn_c_ln_w, L0_attn_Wdt, L0_attn_dt_bias, L0_attn_A, L0_attn_D_param, L0_attn_W_out)
    h = _layernorm(x, axis=-1) * (1 + cb) + sb
    x = x + gb * _L0_ffn_ref(h, L0_ffn_weight, L0_ffn_lora_A, L0_ffn_lora_B, L0_ffn_gw1, L0_ffn_gb1, L0_ffn_ln_gamma, L0_ffn_ln_beta, L0_ffn_gw2, L0_ffn_gb2)
    return x

_drawn_inputs = setup_inputs


def setup_inputs(seed=0):
    import zlib

    import numpy as np

    out = dict(_drawn_inputs(seed))
    spreads = {'L0_attn_dt_ln_w': (1.0, 0.6),
     'L0_attn_b_ln_w': (1.0, 0.6),
     'L0_attn_c_ln_w': (1.0, 0.6),
     'L0_attn_D_param': (1.0, 0.6),
     'L0_ffn_gb1': (0.0, 2.0),
     'L0_ffn_ln_gamma': (1.0, 0.6),
     'L0_ffn_ln_beta': (0.0, 2.0),
     'L0_ffn_gb2': (0.0, 2.0)}
    factors = {'L0_attn_W_in': 8.0,
     'L0_attn_conv_w': 8.0,
     'L0_attn_conv_b': 8.0,
     'L0_attn_Wx': 8.0,
     'L0_attn_Wdt': 8.0,
     'L0_attn_dt_bias': 8.0,
     'L0_attn_A': 8.0,
     'L0_attn_W_out': 8.0,
     'L0_ffn_lora_A': 50.418,
     'L0_ffn_lora_B': 50.714,
     'L0_ffn_gw1': 60.259,
     'L0_ffn_gw2': 64.0,
     'L0_ffn_weight': 8.0}
    for name, (base, spread) in spreads.items():
        noise = np.random.default_rng([zlib.crc32(name.encode()), seed]).standard_normal(out[name].shape)
        drawn = base * np.exp(spread * noise) if base else spread * noise
        out[name] = jnp.asarray(drawn.astype(out[name].dtype))
    for name, factor in factors.items():
        out[name] = (out[name] * factor).astype(out[name].dtype)
    return out
```

```python
from contextlib import ExitStack

import concourse.bass as bass
from concourse import mybir

F32 = mybir.dt.float32
U32 = mybir.dt.uint32
ALU = mybir.AluOpType
ACT = mybir.ActivationFunctionType
AX_X = mybir.AxisListType.X

P = 128
T = 1024
H = 512
D = 1024
NS = 16
R = 32
KW = 4
NE, TOPK, ER, GH = 8, 2, 16, 32
CAP = int(3.0 * T / NE)
ALPHA = 1.0 / ER
RMS_EPS, LN_EPS = 1e-6, 1e-5

TC = 256
CHUNKS = T // TC
TT = TC // P
NT = T // P
KH = H // P
KD = D // P
PAIRS = KD // 2
UNITS = CHUNKS * NS
SLOTS = NS
SIDE = 4
N_DRIVE, N_DECAY, N_BREP = 3, 2, 2
NB = 2
XW = R + 2 * NS
CW, CB, DP, AC = 0, KD * KW, KD * KW + KD, KD * KW + 2 * KD
DCOLS = AC + NS * KD
R_LN, R_GB1, R_GAM, R_BET, R_GB2 = 0, XW, XW + GH, XW + 2 * GH, XW + 3 * GH
ROWS = R_GB2 + NE
SA, CA, GA, SB, CBM, GB = range(6)


def front_slot(slot):
    return {4: ["lnT0", "lnT1"], 5: ["u0"], 6: ["u1"], 7: ["u2"], 8: ["u3"], 10: ["xp"], 11: ["xpT"],
            12: ["dbT"], 13: ["dt0", "dt1", "dt2", "dt3"]}.get(slot, [])


def back_slot(slot):
    return {1: ["y0", "y1", "y2", "y3"], 2: ["g0", "g1"], 3: ["g2", "g3"], 4: ["o0"], 5: ["o1"],
            8: ["l2T0", "l2T1"], 9: ["gh", "la"], 10: ["m0"], 11: ["m1", "ghT"], 12: ["gt"]}.get(slot, [])


def plan_jobs():
    names = ["mod0", "mod1", "modA"]
    for c in range(-1, CHUNKS + 1):
        for slot in range(SLOTS):
            if c > 0:
                names += [f"{j}.{c - 1}" for j in back_slot(slot)]
            if c + 1 < CHUNKS:
                names += [f"{j}.{c + 1}" for j in front_slot(slot)]
            if c == -1 and slot == 8:
                names += ["mod2", "mod3", "mod4", "mod5", "modB"]
    names += ["count"] + [f"lwT{j}" for j in range(2)] + [f"lo{t}" for t in range(NT)]
    return {n: (i % SIDE, i // SIDE + 1) for i, n in enumerate(names)}


def adaln_block(nc, x, w_in_u, w_in_g, dcols_d, w_x, w_dt, w_out, w_ffn, lora_a, lora_b, gw1, gw2,
                rows_d, c_d, w_mod, ident_d, iota_d, out):
    jobs = plan_jobs()
    b_scratch = nc.dram_tensor("b_scratch", (CHUNKS, NS, TC), F32, kind="Internal").ap()
    x2_scratch = nc.dram_tensor("x2_scratch", (T, H), F32, kind="Internal").ap()

    with ExitStack() as ctx:
        def sb(name, shape, dt=F32):
            return ctx.enter_context(nc.sbuf_tensor(name, shape, dt))

        def sem(name):
            return ctx.enter_context(nc.semaphore(name))

        wu = sb("wu", [P, KH, D])
        wg = sb("wg", [P, KH, D])
        wo = sb("wo", [P, KD, H])
        wf = sb("wf", [P, KH, H])
        wla = sb("wla", [P, KH, NE * ER])
        wlb = sb("wlb", [P, H])
        wx = sb("wx", [P, KD, XW])
        wdt = sb("wdt", [R + 1, D])
        wg1 = sb("wg1", [P, KH, GH])
        wg2 = sb("wg2", [GH, NE])
        dcols = sb("dcols", [P, DCOLS])
        rows = sb("rows", [P, ROWS])
        ident = sb("ident", [P, P])
        iota = sb("iota", [P, NE])
        ones = sb("ones", [P, P])
        ccol = sb("ccol", [P, 3, KH])
        mcol = sb("mcol", [P, 4, KH])
        gar = sb("gar", [P, H])
        gbr = sb("gbr", [P, H])
        big = sb("big", [P, 6, KD * TC])
        wmod = big[:, :, :].rearrange("p a b -> p (a b)").rearrange("p (k n) -> p k n", k=KH)
        drive = [big[:, i, :].rearrange("p (d t) -> p d t", d=KD) for i in range(N_DRIVE)]
        acc = big[:, 3, :].rearrange("p (t d) -> p t d", t=TT)
        decay = [big[:, 4 + i, :].rearrange("p (d t) -> p d t", d=KD) for i in range(N_DECAY)]
        x2r = big[:, 0:2, :].rearrange("p a b -> p (a b)").rearrange("p (t h) -> p t h", t=NT)
        lwT = big[:, 4, 0:NT * P].rearrange("p (t n) -> p t n", t=NT)
        lw = big[:, 5, 0:NT * P].rearrange("p (t n) -> p t n", t=NT)
        fin = big[:, 3, :].rearrange("p (b h) -> p b h", h=H)
        xin = sb("xin", [P, TT, H])
        xn = sb("xn", [P, TT, H])
        hT = [sb(f"hT{i}", [P, KH, TC]) for i in range(2)]
        upre = [sb(f"upre{i}", [P, 2, KW - 1 + TC]) for i in range(2)]
        halo = sb("halo", [P, KD, KW - 1])
        xh = sb("xh", [P, KD, TC])
        u = [sb(f"u{i}", [P, KD, TC]) for i in range(2)]
        ssT = upre[0][0:XW, 0, 0:TC]
        bT = upre[1][0:R + NS, 0, 0:TC]
        ghT = upre[1][0:GH, 1, 0:TC]
        ss = sb("ss", [P, TT, XW])
        sq = sb("sq", [P, TT, XW])
        ssn = [sb(f"ssn{i}", [P, TT, XW]) for i in range(2)]
        rinv = sb("rinv", [P, TT, 3])
        dtT = sb("dtT", [R + 1, TC])
        delta = sb("delta", [P, KD, TC])
        du = sb("du", [P, KD, TC])
        brep = [sb(f"brep{i}", [P, NB, TC]) for i in range(N_BREP)]
        carry = sb("carry", [P, NS, KD])
        inj = [sb(f"inj{i}", [P, NS, KD]) for i in range(2)]
        stat = sb("stat", [P, TT, 6])
        mv = sb("mv", [P, TT, 2])
        rstd = sb("rstd", [P, TT, 1])
        mhalf = sb("mhalf", [P, 8])
        xres = sb("xres", [P, TT, H])
        gth = [sb(f"gth{i}", [P, 2, TC]) for i in range(2)]
        h2T = sb("h2T", [P, KH, TC])
        tmp = gth[0][:].rearrange("p i t -> p (i t)")
        mrow = xres[0:1, :, :]
        stat2 = sb("stat2", [P, TT, 6])
        mv2 = sb("mv2", [P, TT, 2])
        rstd2 = sb("rstd2", [P, TT, 1])
        gh = sb("gh", [P, TT, GH])
        gates = sb("gates", [P, TT, NE])
        lt = sb("lt", [P, NT, NE * ER])
        cbc = lt[:, 0:KH, :]
        topv = sb("topv", [P, NT, 8])
        topi = sb("topi", [P, NT, 8], U32)
        idx = sb("idx", [P, NT, TOPK])
        hot = sb("hot", [P, NT, TOPK, NE])
        hotw = big[:, 3, 0:NT * TOPK * NE].rearrange("p (t k e) -> p t k e", k=TOPK, e=NE)
        allowed = sb("allowed", [P, TOPK, NE])
        prob = sb("prob", [P, NT, TOPK])
        ediff = sb("ediff", [P, NT, 2])
        wexp = big[:, 2, 0:NT * NE].rearrange("p (t e) -> p t e", e=NE)

        side = [ctx.enter_context(nc.psum_tensor(f"side{i}", [P, 512], F32)) for i in range(SIDE)]
        stT = [ctx.enter_context(nc.psum_tensor(f"stT{i}", [P, KD * P], F32)) for i in range(2)]

        bank_ready = [sem(f"bank_ready{i}") for i in range(SIDE)]
        bank_free = [sem(f"bank_free{i}") for i in range(SIDE)]
        loads = ["c", "consts", "wm0", "wm1", "wm2", "wu", "wx", "wg", "wo", "wf", "small", "lora"]
        loaded = {n: sem(f"ld_{n}") for n in loads}
        n_load = {}
        xin_loaded, xres_loaded = sem("xin_loaded"), sem("xres_loaded")
        x2_stored, x2_back = sem("x2_stored"), sem("x2_back")
        out_stored = [sem(f"out_stored{i}") for i in range(4)]
        b_stored = sem("b_stored")
        brep_loaded = [sem(f"brep_loaded{i}") for i in range(N_BREP)]
        dve_chain, pool_chain, act_chain = sem("dve_chain"), sem("pool_chain"), sem("act_chain")
        consts_set, c_tanh, c_ready = sem("consts_set"), sem("c_tanh"), sem("c_ready")
        mrow_ready, mcol_ready = sem("mrow_ready"), sem("mcol_ready")
        var_ready, rstd_ready, xn_ready, xin_used = sem("var_ready"), sem("rstd_ready"), sem("xn_ready"), sem("xin_used")
        hT_ready, taps_ready, conv_done, halo_saved = sem("hT_ready"), sem("taps_ready"), sem("conv_done"), sem("halo_saved")
        tanh_ready, u_ready = sem("tanh_ready"), sem("u_ready")
        ssT_ready, ms_ready, rinv_ready, ssn_ready = sem("ssT_ready"), sem("ms_ready"), sem("rinv_ready"), sem("ssn_ready")
        bT_ready, dtT_ready = sem("bT_ready"), sem("dtT_ready")
        log_ready, delta_ready, du_ready = sem("log_ready"), sem("delta_ready"), sem("du_ready")
        first_ready, first_exp = sem("first_ready"), sem("first_exp")
        decay_ready, drive_ready, scanned = sem("decay_ready"), sem("drive_ready"), sem("scanned")
        turned, added, carried, acc_read = sem("turned"), sem("added"), sem("carried"), sem("acc_read")
        gth_ready, z_ready = sem("gth_ready"), sem("z_ready")
        x2_ready = sem("x2_ready")
        h2T_ready, x2m_ready = sem("h2T_ready"), sem("x2m_ready")
        gvar_ready, grstd_ready, gh_ready = sem("gvar_ready"), sem("grstd_ready"), sem("gh_ready")
        ghT_ready = sem("ghT_ready")
        lt_ready, hot_ready, diff_ready, ediff_ready = sem("lt_ready"), sem("hot_ready"), sem("diff_ready"), sem("ediff_ready")
        lw_ready, lwT_ready, fin_ready = sem("lw_ready"), sem("lwT_ready"), sem("fin_ready")

        def psum(name):
            return side[jobs[name][0]]

        def wait_job(eng, name):
            bank, nth = jobs[name]
            eng.wait_ge(bank_ready[bank], nth)

        def free(name):
            return bank_free[jobs[name][0]]

        class Chain:

            def __init__(self, eng, s):
                self.eng, self.s, self.n = eng, s, 0

            def __call__(self, ins):
                self.n += 1
                ins.then_inc(self.s, 1)
                self.eng.wait_ge(self.s, self.n)

        def wait_load(eng, name):
            eng.wait_ge(loaded[name], 16 * n_load[name])

        def xn_front(c):
            return TT * (c + 1 + max(0, c - 2))

        def xn_back(c):
            return TT * (min(c + 3, CHUNKS) + c + 1)

        def slots():
            for c in range(-1, CHUNKS + 1):
                for slot in range(SLOTS):
                    yield c, slot

        def in_front(c):
            return c + 1 < CHUNKS

        def in_back(c):
            return c > 0

        def wait_mod_done(eng):
            for r in range(2, 6):
                wait_job(eng, f"mod{r}")

        block = ctx.enter_context(nc.Block())

        @block.sync
        def _(sp):
            def load(group, dst, src):
                n_load[group] = n_load.get(group, 0) + 1
                sp.dma_start(dst, src).then_inc(loaded[group], 16)

            load("c", ccol[:, 0, :], c_d)
            load("wm0", wmod[:, :, 0:1024], w_mod[:, :, 0:1024])
            xt = x.rearrange("(c t p) h -> c p t h", p=P, t=TT)
            sp.dma_start(xin[:], xt[0]).then_inc(xin_loaded, 16)
            load("consts", ident[:], ident_d)
            load("consts", iota[:], iota_d)
            load("consts", dcols[:], dcols_d)
            load("consts", rows[:], rows_d.broadcast_to([P, ROWS]))
            load("wu", wu[:], w_in_u)
            load("wx", wx[:], w_x)
            load("wx", wdt[:], w_dt)
            load("wm1", wmod[:, :, 1024:2048], w_mod[:, :, 1024:2048])
            load("wm2", wmod[:, :, 2048:3072], w_mod[:, :, 2048:3072])

            for c, slot in slots():
                if in_front(c) and slot == 0 and c >= 0:
                    sp.wait_ge(xin_used, c + 1)
                    sp.dma_start(xin[:], xt[c + 1]).then_inc(xin_loaded, 16)
                if in_back(c) and slot == 0:
                    if c >= 2:
                        sp.wait_ge(x2_stored, 16 * (c - 1))
                    sp.dma_start(xres[:], xt[c - 1]).then_inc(xres_loaded, 16)
                if in_front(c) and slot == 12:
                    sp.wait_ge(bT_ready, c + 2)
                    sp.dma_start(b_scratch[c + 1], bT[R:R + NS, :]).then_inc(b_stored, 16)
                g = c * NS + slot + 2
                if g % NB == 0 and 0 <= g < UNITS:
                    j = g // NB
                    if g % NS == 0:
                        sp.wait_ge(b_stored, 16 * (g // NS + 1))
                    if j >= N_BREP:
                        sp.wait_ge(drive_ready, NB * (j - N_BREP) + NB)
                    cc, n = g // NS, g % NS
                    src = b_scratch[cc:cc + 1, n:n + NB, :].broadcast_to([P, NB, TC])
                    sp.dma_start(brep[j % N_BREP][:], src).then_inc(brep_loaded[j % N_BREP], 16)
                if c == -1 and slot == 15:
                    load("wg", wg[:], w_in_g)
                    load("wo", wo[:], w_out)
                    load("wf", wf[:], w_ffn)
                    load("small", wg1[:], gw1)
                    load("small", wg2[:], gw2)
                    load("lora", wla[:], lora_a)
                    load("lora", wlb[:], lora_b)
                if in_back(c) and slot == 12:
                    sp.wait_ge(x2m_ready, TT * c)
                    sp.dma_start(x2_scratch.rearrange("(c t p) h -> c p t h", p=P, t=TT)[c - 1],
                                 xres[:]).then_inc(x2_stored, 16)
            sp.wait_ge(x2_stored, 16 * CHUNKS)
            sp.wait_ge(turned, TT * UNITS)
            sp.wait_ge(carried, UNITS - NS)
            sp.dma_start(x2r[:], x2_scratch.rearrange("(t p) h -> p t h", p=P)).then_inc(x2_back, 16)
            for t in range(NT):
                sp.wait_ge(fin_ready, t + 1)
                sp.dma_start(out[t * P:(t + 1) * P, :], fin[:, t % 4, :]).then_inc(out_stored[t % 4], 16)
            for i in range(4):
                sp.wait_ge(out_stored[i], 16 * NT // 4)

        @block.tensor
        def _(pe):
            def begin(name):
                bank, nth = jobs[name]
                if nth > 1:
                    pe.wait_ge(bank_free[bank], nth - 1)
                return side[bank]

            def end(name, ins):
                ins.then_inc(bank_ready[jobs[name][0]], 1)

            def mod_row(r):
                ps = begin(f"mod{r}")
                wait_load(pe, f"wm{r // 2}")
                for k in range(KH):
                    last = pe.matmul(ps[:, :], cbc[:, k, :], wmod[:, k, r * H:(r + 1) * H],
                                     start=(k == 0), stop=(k == KH - 1))
                end(f"mod{r}", last)

            def mod_cols(name, n_rows):
                ps = begin(name)
                pe.wait_ge(mrow_ready, n_rows)
                for i in range(2):
                    for k in range(KH):
                        last = pe.matmul(ps[:, i * KH + k:i * KH + k + 1], mrow[0:1, i, k * P:(k + 1) * P],
                                         ones[0:1, 0:1], start=True, stop=True)
                end(name, last)

            def turn_tokens(job, src):
                for j in range(2):
                    ps = begin(job(j))
                    for k in range(2):
                        for t in range(TT):
                            f = (2 * j + k) * P
                            last = pe.transpose(ps[:, k * TC + t * P:k * TC + (t + 1) * P],
                                                src[:, t, f:f + P], ident[:])
                    end(job(j), last)

            def project_pair(name, weights, q, rhs):
                ps = begin(name)
                for i in range(2):
                    d0 = (2 * q + i) * P
                    for k in range(KH):
                        last = pe.matmul(ps[:, i * TC:(i + 1) * TC], weights[:, k, d0:d0 + P], rhs[:, k, :],
                                         start=(k == 0), stop=(k == KH - 1))
                end(name, last)

            def front(c, slot):
                if slot == 4:
                    pe.wait_ge(xn_ready, xn_front(c))
                    turn_tokens(lambda j: f"lnT{j}.{c}", xn)
                if 5 <= slot <= 8:
                    pe.wait_ge(hT_ready, KH * (c + 1))
                    project_pair(f"u{slot - 5}.{c}", wu, slot - 5, hT[c % 2])
                if slot == 10:
                    ps = begin(f"xp.{c}")
                    pe.wait_ge(u_ready, 2 * (c + 1))
                    for k in range(KD):
                        last = pe.matmul(ps[0:XW, 0:TC], wx[:, k, :], u[c % 2][:, k, :],
                                         start=(k == 0), stop=(k == KD - 1))
                    end(f"xp.{c}", last)
                if slot == 11:
                    ps = begin(f"xpT.{c}")
                    pe.wait_ge(ssT_ready, c + 1)
                    for t in range(TT):
                        last = pe.transpose(ps[:, t * XW:(t + 1) * XW], ssT[:, t * P:(t + 1) * P],
                                            ident[0:XW, 0:XW])
                    end(f"xpT.{c}", last)
                if slot == 12:
                    ps = begin(f"dbT.{c}")
                    pe.wait_ge(ssn_ready, c + 1)
                    for t in range(TT):
                        last = pe.transpose(ps[0:R + NS, t * P:(t + 1) * P], ssn[c % 2][:, t, 0:R + NS], ident[:])
                    end(f"dbT.{c}", last)
                if slot == 13:
                    pe.wait_ge(dtT_ready, c + 1)
                    for q in range(PAIRS):
                        ps = begin(f"dt{q}.{c}")
                        for i in range(2):
                            d0 = (2 * q + i) * P
                            last = pe.matmul(ps[:, i * TC:(i + 1) * TC], wdt[:, d0:d0 + P], dtT[:, :],
                                             start=True, stop=True)
                        end(f"dt{q}.{c}", last)

            def back(c, slot):
                if slot == 1:
                    pe.wait_ge(added, TT * NS * (c + 1))
                    for q in range(PAIRS):
                        ps = begin(f"y{q}.{c}")
                        for i in range(2):
                            for t in range(TT):
                                d0 = (2 * q + i) * P
                                last = pe.transpose(ps[:, i * TC + t * P:i * TC + (t + 1) * P],
                                                    acc[:, t, d0:d0 + P], ident[:])
                        end(f"y{q}.{c}", last)
                if slot in (2, 3):
                    wait_load(pe, "wg")
                    for q in (2 * slot - 4, 2 * slot - 3):
                        project_pair(f"g{q}.{c}", wg, q, hT[c % 2])
                if slot in (4, 5):
                    t = slot - 4
                    ps = begin(f"o{t}.{c}")
                    wait_load(pe, "wo")
                    pe.wait_ge(z_ready, PAIRS * (c + 1))
                    for k in range(KD):
                        last = pe.matmul(ps[:, :], u[c % 2][:, k, t * P:(t + 1) * P], wo[:, k, :],
                                         start=(k == 0), stop=(k == KD - 1))
                    end(f"o{t}.{c}", last)
                if slot == 8:
                    pe.wait_ge(xn_ready, xn_back(c))
                    turn_tokens(lambda j: f"l2T{j}.{c}", xn)
                if slot == 9:
                    ps = begin(f"gh.{c}")
                    pe.wait_ge(h2T_ready, KH * (c + 1))
                    wait_load(pe, "small")
                    wait_load(pe, "lora")
                    for t in range(TT):
                        for k in range(KH):
                            last = pe.matmul(ps[:, t * GH:(t + 1) * GH], h2T[:, k, t * P:(t + 1) * P],
                                             wg1[:, k, :], start=(k == 0), stop=(k == KH - 1))
                    end(f"gh.{c}", last)
                    ps = begin(f"la.{c}")
                    for t in range(TT):
                        for k in range(KH):
                            last = pe.matmul(ps[:, t * P:(t + 1) * P], h2T[:, k, t * P:(t + 1) * P],
                                             wla[:, k, :], start=(k == 0), stop=(k == KH - 1))
                    end(f"la.{c}", last)
                if slot in (10, 11):
                    t = slot - 10
                    ps = begin(f"m{t}.{c}")
                    wait_load(pe, "wf")
                    for k in range(KH):
                        last = pe.matmul(ps[:, :], h2T[:, k, t * P:(t + 1) * P], wf[:, k, :],
                                         start=(k == 0), stop=(k == KH - 1))
                    end(f"m{t}.{c}", last)
                if slot == 11:
                    ps = begin(f"ghT.{c}")
                    pe.wait_ge(gh_ready, c + 1)
                    for t in range(TT):
                        last = pe.transpose(ps[0:GH, t * P:(t + 1) * P], gh[:, t, :], ident[:])
                    end(f"ghT.{c}", last)
                if slot == 12:
                    ps = begin(f"gt.{c}")
                    pe.wait_ge(ghT_ready, c + 1)
                    for t in range(TT):
                        last = pe.matmul(ps[:, t * NE:(t + 1) * NE], ghT[:, t * P:(t + 1) * P], wg2[:, :],
                                         start=True, stop=True)
                    end(f"gt.{c}", last)

            pe.wait_ge(consts_set, 1)
            wait_load(pe, "consts")
            pe.wait_ge(c_ready, 1)
            mod_row(SA)
            mod_row(CA)
            mod_cols("modA", 2)
            wait_load(pe, "wu")
            wait_load(pe, "wx")
            for c, slot in slots():
                if in_back(c):
                    back(c - 1, slot)
                if in_front(c):
                    front(c + 1, slot)
                if c == -1 and slot == 8:
                    for r in (GA, SB, CBM, GB):
                        mod_row(r)
                    mod_cols("modB", 4)
                if 0 <= c < CHUNKS:
                    g = c * NS + slot
                    for t in range(TT):
                        k = TT * g + t
                        pe.wait_ge(scanned, g + 1)
                        if k >= 2:
                            pe.wait_ge(added, k - 1)
                        for d in range(KD):
                            last = pe.transpose(stT[k % 2][:, d * P:(d + 1) * P],
                                                drive[g % N_DRIVE][:, d, t * P:(t + 1) * P], ident[:])
                        last.then_inc(turned, 1)
            ps = begin("count")
            pe.wait_ge(hot_ready, 1)
            for t in range(NT):
                last = pe.matmul(ps[:, 0:TOPK * NE], ones[:], hot[:, t, :, :].rearrange("p k e -> p (k e)"),
                                 start=(t == 0), stop=(t == NT - 1))
            end("count", last)
            pe.wait_ge(lw_ready, 1)
            for j in range(2):
                ps = begin(f"lwT{j}")
                for i in range(NT // 2):
                    last = pe.transpose(ps[:, i * P:(i + 1) * P], lw[:, j * NT // 2 + i, :], ident[:])
                end(f"lwT{j}", last)
            for t in range(NT):
                ps = begin(f"lo{t}")
                pe.wait_ge(lwT_ready, t // (NT // 2) + 1)
                end(f"lo{t}", pe.matmul(ps[:, :], lwT[:, t, :], wlb[:, :], start=True, stop=True))

        @block.scalar
        def _(act):
            def evacuate_norm(job, dst, shift, ready):
                for j in range(2):
                    wait_job(act, job(j))
                    for i in range(2):
                        k = 2 * j + i
                        ins = act.activation(dst[:, k, :], psum(job(j))[:, i * TC:(i + 1) * TC], ACT.Identity,
                                             bias=mcol[:, shift, k:k + 1], scale=mcol[:, shift + 1, k:k + 1])
                        ins.then_inc(ready, 1)
                    act.wait_ge(ready, evacuate_norm.n + 2 * j + 2)
                    act.sem_inc(free(job(j)), 1)

            def front(c, slot):
                if slot == 4:
                    if c == 0:
                        act.wait_ge(mcol_ready, 1)
                    evacuate_norm.n = KH * c
                    evacuate_norm(lambda j: f"lnT{j}.{c}", hT[c % 2], 0, hT_ready)
                if 5 <= slot <= 8:
                    q = slot - 5
                    name = f"u{q}.{c}"
                    if c == 0 and q == 0:
                        act.wait_ge(c_ready, 2)
                    wait_job(act, name)
                    if c >= 1 and q == 1:
                        act.wait_ge(b_stored, 16 * c)
                    if 4 * c + q >= 2:
                        act.wait_ge(conv_done, 4 * c + q - 1)
                        act.wait_ge(halo_saved, 4 * c + q - 1)
                    act.activation(upre[q % 2][:, :, KW - 1:], psum(name)[:, :].rearrange("p (i t) -> p i t", i=2),
                                   ACT.Copy).then_inc(taps_ready, 1)
                    for i in range(2):
                        d = 2 * q + i
                        ins = act.activation(xh[:, d, :], psum(name)[:, i * TC:(i + 1) * TC], ACT.Identity,
                                             bias=dcols[:, CB + d:CB + d + 1],
                                             scale=dcols[:, CW + d * KW + KW - 1:CW + d * KW + KW])
                        ins.then_inc(taps_ready, 1)
                    act.wait_ge(taps_ready, 3 * (4 * c + q + 1))
                    act.sem_inc(free(name), 1)
                if slot == 9:
                    act.wait_ge(conv_done, 4 * (c + 1))
                    for j in range(2):
                        act.activation(u[c % 2][:, 4 * j:4 * j + 4, :], xh[:, 4 * j:4 * j + 4, :],
                                       ACT.Tanh).then_inc(tanh_ready, 1)
                if slot == 10:
                    wait_job(act, f"xp.{c}")
                    act.wait_ge(halo_saved, 4 * (c + 1))
                    act.activation(ssT[:, :], psum(f"xp.{c}")[0:XW, 0:TC], ACT.Copy).then_inc(ssT_ready, 1)
                    act.wait_ge(ssT_ready, c + 1)
                    act.sem_inc(free(f"xp.{c}"), 1)
                if slot == 12:
                    name = f"dbT.{c}"
                    wait_job(act, name)
                    if c >= 1:
                        act.wait_ge(b_stored, 16 * c)
                    act.activation(dtT[0:R, :], psum(name)[0:R, 0:TC], ACT.Copy).then_inc(dtT_ready, 1)
                    act.activation(bT[R:R + NS, :], psum(name)[R:R + NS, 0:TC], ACT.Copy).then_inc(bT_ready, 1)
                    act.wait_ge(dtT_ready, c + 1)
                    act.wait_ge(bT_ready, c + 1)
                    act.sem_inc(free(name), 1)
                if slot == 13:
                    act.wait_ge(u_ready, 2 * (c + 1))
                    log = xh[:, :, :].rearrange("p d t -> p (d t)")
                    for q in range(PAIRS):
                        wait_job(act, f"dt{q}.{c}")
                        ins = act.activation(log[:, q * 512:(q + 1) * 512], psum(f"dt{q}.{c}")[:, :], ACT.Abs)
                        ins.then_inc(act_chain, 1)
                    act.wait_ge(act_chain, 5 * c + 4)
                    act.activation(log, log, ACT.Exp, scale=-1.0).then_inc(act_chain, 1)
                    act.wait_ge(act_chain, 5 * c + 5)
                    act.activation(log, log, ACT.Ln, bias=1.0).then_inc(log_ready, 1)
                if slot == 15 and c >= 1:
                    act.wait_ge(first_ready, c)
                    act.activation(inj[c % 2][:], inj[c % 2][:], ACT.Exp).then_inc(first_exp, 1)

            def back(c, slot):
                if slot in (2, 3):
                    for q in (2 * slot - 4, 2 * slot - 3):
                        wait_job(act, f"g{q}.{c}")
                        if 4 * c + q >= 2:
                            act.wait_ge(z_ready, 4 * c + q - 1)
                        act.activation(gth[q % 2][:].rearrange("p i t -> p (i t)"), psum(f"g{q}.{c}")[:, :],
                                       ACT.Tanh, scale=0.5).then_inc(gth_ready, 1)
                if slot == 8:
                    if c == 0:
                        act.wait_ge(mcol_ready, 2)
                    evacuate_norm.n = KH * c
                    evacuate_norm(lambda j: f"l2T{j}.{c}", h2T, 2, h2T_ready)
                if slot == 9:
                    wait_job(act, f"la.{c}")
                    act.activation(lt[:, TT * c:TT * c + TT, :].rearrange("p t n -> p (t n)"),
                                   psum(f"la.{c}")[:, 0:TT * P], ACT.Copy).then_inc(lt_ready, 1)
                    act.wait_ge(lt_ready, c + 1)
                    act.sem_inc(free(f"la.{c}"), 1)
                if slot == 11:
                    wait_job(act, f"ghT.{c}")
                    act.activation(ghT[:, :], psum(f"ghT.{c}")[0:GH, 0:TC], ACT.Copy).then_inc(ghT_ready, 1)
                    act.wait_ge(ghT_ready, c + 1)
                    act.sem_inc(free(f"ghT.{c}"), 1)

            wait_load(act, "c")
            act.activation(ccol[:, 1, :], ccol[:, 0, :], ACT.Tanh, scale=0.5).then_inc(c_tanh, 1)

            def mod_row_out(r, i, n):
                wait_job(act, f"mod{r}")
                act.activation(mrow[0:1, i, :], psum(f"mod{r}")[0:1, :], ACT.Copy,
                               ).then_inc(mrow_ready, 1)
                act.wait_ge(mrow_ready, n)
                act.sem_inc(free(f"mod{r}"), 1)

            mod_row_out(SA, 0, 1)
            mod_row_out(CA, 1, 2)
            for c, slot in slots():
                if in_back(c):
                    back(c - 1, slot)
                if in_front(c):
                    front(c + 1, slot)
                if c == -1 and slot == 8:
                    act.wait_ge(mcol_ready, 1)
                    mod_row_out(SB, 0, 3)
                    mod_row_out(CBM, 1, 4)
                g = c * NS + slot + 2
                if 0 <= g < UNITS:
                    cc, n = g // NS, g % NS
                    if g == 0:
                        act.wait_ge(consts_set, 2)
                    if n == 0:
                        act.wait_ge(delta_ready, PAIRS * (cc + 1))
                    if g >= N_DECAY:
                        act.wait_ge(scanned, g - N_DECAY + 1)
                    for d in range(KD):
                        ins = act.activation(decay[g % N_DECAY][:, d, 1:], delta[:, d, 1:], ACT.Exp,
                                             scale=dcols[:, AC + n * KD + d:AC + n * KD + d + 1])
                    ins.then_inc(decay_ready, 1)
            act.wait_ge(diff_ready, 1)
            act.activation(ediff[:, :, 1:2], ediff[:, :, 0:1], ACT.Exp).then_inc(ediff_ready, 1)
            act.wait_ge(decay_ready, UNITS)
            for j in range(2):
                wait_job(act, f"lwT{j}")
                half = NT // 2
                act.activation(lwT[:, j * half:(j + 1) * half, :].rearrange("p t n -> p (t n)"),
                               psum(f"lwT{j}")[:, :], ACT.Copy).then_inc(lwT_ready, 1)
                act.wait_ge(lwT_ready, j + 1)
                act.sem_inc(free(f"lwT{j}"), 1)

        @block.gpsimd
        def _(pool):
            chain = Chain(pool, pool_chain)
            pool.memset(mhalf[:], -0.5)
            chain(pool.memset(halo[:], 0.0))
            chain(pool.memset(dtT[R:R + 1, :], 1.0))
            chain(pool.memset(ones[:], 1.0))
            pool.sem_inc(consts_set, 1)
            n_var = 0

            def rsqrt(dst, src, n, done):
                pool.tensor_tensor(dst, src, mhalf[:, 0:n].rearrange("p (t o) -> p t o", t=TT),
                                   ALU.pow).then_inc(done, 1)

            for c, slot in slots():
                if in_front(c) and slot == 3:
                    n_var += 1
                    pool.wait_ge(var_ready, n_var)
                    rsqrt(rstd[:], rstd[:], TT, rstd_ready)
                if in_front(c) and slot == 11:
                    pool.wait_ge(ms_ready, c + 2)
                    rsqrt(rinv[:], rinv[:], 3 * TT, rinv_ready)
                if in_back(c) and slot == 6:
                    n_var += 1
                    pool.wait_ge(var_ready, n_var)
                    rsqrt(rstd[:], rstd[:], TT, rstd_ready)
                if in_back(c) and slot == 10:
                    pool.wait_ge(gvar_ready, c)
                    rsqrt(rstd2[:], rstd2[:], TT, grstd_ready)
                if in_front(c) and slot == 14:
                    if c >= 0:
                        pool.wait_ge(drive_ready, NS * (c + 1))
                    pool.wait_ge(delta_ready, PAIRS * (c + 2))
                    pool.wait_ge(u_ready, 2 * (c + 2))
                    pool.tensor_tensor(du[:], delta[:], u[(c + 1) % 2][:], ALU.mult).then_inc(du_ready, 1)
                g = c * NS + slot + 2
                if 0 <= g < UNITS:
                    j = g // NB
                    if g == 0:
                        wait_mod_done(pool)
                        for i in range(N_DECAY):
                            chain(pool.memset(decay[i][:, :, 0:1], 0.0))
                        pool.sem_inc(consts_set, 1)
                    if g % NS == 0:
                        pool.wait_ge(du_ready, g // NS + 1)
                    pool.wait_ge(brep_loaded[j % N_BREP], 16 * (j // N_BREP + 1))
                    if g >= N_DRIVE:
                        pool.wait_ge(turned, TT * (g - N_DRIVE + 1))
                        if g - N_DRIVE < UNITS - NS:
                            pool.wait_ge(carried, g - N_DRIVE + 1)
                    pool.tensor_tensor(drive[g % N_DRIVE], du[:],
                                       brep[j % N_BREP][:, g % NB:g % NB + 1, :].broadcast_to([P, KD, TC]),
                                       ALU.mult).then_inc(drive_ready, 1)

        @block.vector
        def _(dve):
            chain = Chain(dve, dve_chain)
            state = {"var": 0}

            def norm_stats(src):
                for t in range(TT):
                    ins = dve.bn_stats(stat[:, t, :], src[:, t, :])
                chain(ins)
                for t in range(TT):
                    ins = dve.bn_aggr(mv[:, t, :], stat[:, t, :])
                chain(ins)
                dve.tensor_scalar(rstd[:], mv[:, :, 1:2], LN_EPS, None, ALU.add).then_inc(var_ready, 1)
                state["var"] += 1

            def normalise(src):
                dve.wait_ge(rstd_ready, state["var"])
                for t in range(TT):
                    ins = dve.tensor_scalar(xn[:, t, :], src[:, t, :], mv[:, t, 0:1], rstd[:, t, :],
                                            ALU.subtract, ALU.mult)
                    ins.then_inc(xn_ready, 1)

            def front(c, slot):
                if slot == 3:
                    dve.wait_ge(xin_loaded, 16 * (c + 1))
                    norm_stats(xin)
                    if c >= 1:
                        for j in range(2):
                            wait_job(dve, f"l2T{j}.{c - 3}" if c >= 3 else f"lnT{j}.{c - 1}")
                    normalise(xin)
                    dve.wait_ge(xn_ready, xn_front(c))
                    dve.sem_inc(xin_used, 1)
                if 5 <= slot <= 8:
                    q = slot - 5
                    pre = upre[q % 2]
                    dve.wait_ge(taps_ready, 3 * (4 * c + q + 1))
                    chain(dve.tensor_copy(pre[:, :, 0:KW - 1], halo[:, 2 * q:2 * q + 2, :]))
                    for tap in range(KW - 1):
                        for i in range(2):
                            d = 2 * q + i
                            ins = dve.scalar_tensor_tensor(
                                out=xh[:, d, :], in0=pre[:, i, tap:tap + TC],
                                scalar=dcols[:, CW + d * KW + tap:CW + d * KW + tap + 1],
                                in1=xh[:, d, :], op0=ALU.mult, op1=ALU.add)
                            if tap == KW - 2:
                                break
                        if tap < KW - 2:
                            chain(ins)
                    d = 2 * q + 1
                    chain(ins)
                    dve.scalar_tensor_tensor(
                        out=xh[:, d, :], in0=pre[:, 1, KW - 2:KW - 2 + TC],
                        scalar=dcols[:, CW + d * KW + KW - 2:CW + d * KW + KW - 1],
                        in1=xh[:, d, :], op0=ALU.mult, op1=ALU.add).then_inc(conv_done, 1)
                    dve.tensor_copy(halo[:, 2 * q:2 * q + 2, :], pre[:, :, TC:TC + KW - 1]).then_inc(halo_saved, 1)
                if slot == 9:
                    for j in range(2):
                        dve.wait_ge(tanh_ready, 2 * c + j + 1)
                        s = slice(4 * j, 4 * j + 4)
                        flat = lambda a: a[:, s, :].rearrange("p d t -> p (d t)")
                        dve.scalar_tensor_tensor(out=flat(u[c % 2]), in0=flat(u[c % 2]), scalar=1.0,
                                                 in1=flat(xh), op0=ALU.add, op1=ALU.mult).then_inc(u_ready, 1)
                if slot == 11:
                    name = f"xpT.{c}"
                    wait_job(dve, name)
                    chain(dve.tensor_copy(ss[:].rearrange("p t n -> p (t n)"), psum(name)[:, 0:TT * XW]))
                    dve.sem_inc(free(name), 1)
                    chain(dve.tensor_tensor(sq[:], ss[:], ss[:], ALU.mult))
                    dve.tensor_reduce(rinv[:, :, 0], sq[:, :, 0:R], AX_X, ALU.add)
                    chain(dve.tensor_reduce(rinv[:, :, 1:3],
                                            sq[:, :, R:].rearrange("p t (g n) -> p t g n", n=NS), AX_X, ALU.add))
                    dve.tensor_scalar(rinv[:, :, 0], rinv[:, :, 0], 1.0 / R, RMS_EPS, ALU.mult, ALU.add)
                    chain(dve.tensor_scalar(rinv[:, :, 1:3], rinv[:, :, 1:3], 1.0 / NS, RMS_EPS, ALU.mult, ALU.add))
                    dve.sem_inc(ms_ready, 1)
                    dve.wait_ge(rinv_ready, c + 1)
                    for t in range(TT):
                        for g, (a, b) in enumerate(((0, R), (R, R + NS), (R + NS, XW))):
                            ins = dve.scalar_tensor_tensor(
                                out=ssn[c % 2][:, t, a:b], in0=ss[:, t, a:b], scalar=rinv[:, t, g:g + 1],
                                in1=rows[:, R_LN + a:R_LN + b], op0=ALU.mult, op1=ALU.mult)
                    ins.then_inc(ssn_ready, 1)
                if slot == 14:
                    dve.wait_ge(log_ready, c + 1)
                    if c >= 1:
                        dve.wait_ge(decay_ready, NS * c)
                    for q in range(PAIRS):
                        ins = dve.scalar_tensor_tensor(
                            out=delta[:, 2 * q:2 * q + 2, :].rearrange("p d t -> p (d t)"),
                            in0=psum(f"dt{q}.{c}")[:, :], scalar=0.0,
                            in1=xh[:, 2 * q:2 * q + 2, :].rearrange("p d t -> p (d t)"),
                            op0=ALU.max, op1=ALU.add)
                        ins.then_inc(delta_ready, 1)
                    for q in range(PAIRS):
                        dve.wait_ge(delta_ready, PAIRS * c + q + 1)
                        dve.sem_inc(free(f"dt{q}.{c}"), 1)
                    if c >= 1:
                        dve.tensor_tensor(inj[c % 2][:], dcols[:, AC:AC + NS * KD].rearrange("p (n d) -> p n d", n=NS),
                                          delta[:, :, 0:1].rearrange("p d o -> p o d").broadcast_to([P, NS, KD]),
                                          ALU.mult).then_inc(first_ready, 1)

            def back(c, slot):
                uc = u[c % 2]
                if slot == 1:
                    for q in range(PAIRS):
                        wait_job(dve, f"y{q}.{c}")
                        for i in range(2):
                            d = 2 * q + i
                            ins = dve.scalar_tensor_tensor(
                                out=uc[:, d, :], in0=uc[:, d, :], scalar=dcols[:, DP + d:DP + d + 1],
                                in1=psum(f"y{q}.{c}")[:, i * TC:(i + 1) * TC], op0=ALU.mult, op1=ALU.add)
                            if i == 0:
                                continue
                        chain(ins)
                        dve.sem_inc(free(f"y{q}.{c}"), 1)
                if slot in (2, 3):
                    for q in (2 * slot - 4, 2 * slot - 3):
                        dve.wait_ge(gth_ready, 4 * c + q + 1)
                        g2 = gth[q % 2][:].rearrange("p i t -> p (i t)")
                        chain(dve.scalar_tensor_tensor(out=g2, in0=g2, scalar=1.0, in1=psum(f"g{q}.{c}")[:, :],
                                                       op0=ALU.add, op1=ALU.mult))
                        dve.sem_inc(free(f"g{q}.{c}"), 1)
                        z = uc[:, 2 * q:2 * q + 2, :].rearrange("p i t -> p (i t)")
                        dve.scalar_tensor_tensor(out=z, in0=g2, scalar=0.5, in1=z,
                                                 op0=ALU.mult, op1=ALU.mult).then_inc(z_ready, 1)
                if slot in (5, 6):
                    t = slot - 5
                    name = f"o{t}.{c}"
                    wait_job(dve, name)
                    if t == 0:
                        dve.wait_ge(xres_loaded, 16 * (c + 1))
                    chain(dve.tensor_tensor(tmp, gar[:], psum(name)[:, :], ALU.mult))
                    dve.sem_inc(free(name), 1)
                    chain(dve.tensor_tensor(xres[:, t, :], xres[:, t, :], tmp, ALU.add))
                if slot == 6:
                    norm_stats(xres)
                if slot == 7:
                    for j in range(2):
                        wait_job(dve, f"lnT{j}.{c + 2}" if c + 2 < CHUNKS else f"l2T{j}.{c - 1}")
                    normalise(xres)
                if slot == 10:
                    name = f"gh.{c}"
                    wait_job(dve, name)
                    chain(dve.tensor_tensor(gh[:], rows[:, None, R_GB1:R_GB1 + GH].broadcast_to([P, TT, GH]),
                                            psum(name)[:, 0:TT * GH].rearrange("p (t n) -> p t n", t=TT), ALU.add))
                    dve.sem_inc(free(name), 1)
                    for t in range(TT):
                        ins = dve.bn_stats(stat2[:, t, :], gh[:, t, :])
                    chain(ins)
                    for t in range(TT):
                        ins = dve.bn_aggr(mv2[:, t, :], stat2[:, t, :])
                    chain(ins)
                    dve.tensor_scalar(rstd2[:], mv2[:, :, 1:2], LN_EPS, None, ALU.add).then_inc(gvar_ready, 1)
                    dve.wait_ge(grstd_ready, c + 1)
                    for t in range(TT):
                        ins = dve.tensor_scalar(gh[:, t, :], gh[:, t, :], mv2[:, t, 0:1], rstd2[:, t, :],
                                                ALU.subtract, ALU.mult)
                    chain(ins)
                    chain(dve.tensor_tensor(gh[:], gh[:], rows[:, None, R_GAM:R_GAM + GH].broadcast_to([P, TT, GH]),
                                            ALU.mult))
                    chain(dve.tensor_tensor(gh[:], gh[:], rows[:, None, R_BET:R_BET + GH].broadcast_to([P, TT, GH]),
                                            ALU.add))
                    dve.tensor_scalar(gh[:], gh[:], 0.0, None, ALU.max).then_inc(gh_ready, 1)
                if slot in (11, 12):
                    t = slot - 11
                    name = f"m{t}.{c}"
                    wait_job(dve, name)
                    if t > 0:
                        dve.wait_ge(x2m_ready, TT * c + t)
                    chain(dve.tensor_tensor(tmp, gbr[:], psum(name)[:, :], ALU.mult))
                    dve.sem_inc(free(name), 1)
                    dve.tensor_tensor(xres[:, t, :], xres[:, t, :], tmp, ALU.add).then_inc(x2m_ready, 1)
                if slot == 13:
                    name = f"gt.{c}"
                    wait_job(dve, name)
                    chain(dve.tensor_tensor(gates[:], rows[:, None, R_GB2:R_GB2 + NE].broadcast_to([P, TT, NE]),
                                            psum(name)[:, 0:TT * NE].rearrange("p (t n) -> p t n", t=TT), ALU.add))
                    dve.sem_inc(free(name), 1)
                    for t in range(TT):
                        ins = dve.max(topv[:, TT * c + t, :], gates[:, t, :])
                    chain(ins)
                    for t in range(TT):
                        ins = dve.max_index(topi[:, TT * c + t, :], topv[:, TT * c + t, :], gates[:, t, :])
                    chain(ins)

            def keep_last(g):
                if g < UNITS - NS:
                    dve.wait_ge(scanned, g + 1)
                    dve.tensor_copy(carry[:, g % NS, :].rearrange("p (d o) -> p d o", o=1),
                                    drive[g % N_DRIVE][:, :, TC - 1:TC]).then_inc(carried, 1)

            def scan(g):
                dve.wait_ge(decay_ready, g + 1)
                dve.wait_ge(drive_ready, g + 1)
                v = drive[g % N_DRIVE]
                if g >= NS:
                    chain(dve.tensor_tensor(v[:, :, 0:1], v[:, :, 0:1],
                                            inj[g // NS % 2][:, g % NS, :].rearrange("p (d o) -> p d o", o=1), ALU.add))
                flat = v.rearrange("p d t -> p (d t)")
                dve.tensor_tensor_scan(flat, decay[g % N_DECAY].rearrange("p d t -> p (d t)"), flat, 0.0,
                                       ALU.mult, ALU.add).then_inc(scanned, 1)

            def add_states(g):
                c, n = g // NS, g % NS
                for t in range(TT):
                    k = TT * g + t
                    dve.wait_ge(turned, k + 1)
                    cn = ssn[c % 2][:, t, R + NS + n:R + NS + n + 1]
                    if n == 0:
                        if t == 0 and c >= 1:
                            for q in range(PAIRS):
                                wait_job(dve, f"y{q}.{c - 1}")
                        dve.tensor_scalar(acc[:, t, :], stT[k % 2][:], cn, None, ALU.mult).then_inc(added, 1)
                    else:
                        dve.wait_ge(added, k - 1)
                        dve.scalar_tensor_tensor(out=acc[:, t, :], in0=stT[k % 2][:], scalar=cn, in1=acc[:, t, :],
                                                 op0=ALU.mult, op1=ALU.add).then_inc(added, 1)

            def gate_row(r, dst):
                wait_job(dve, f"mod{r}")
                ps = psum(f"mod{r}")
                chain(dve.tensor_scalar(dst[:], ps[:, :], 0.0, 2.0, ALU.is_ge, ALU.mult))
                chain(dve.tensor_scalar(dst[:], dst[:], -1.0, None, ALU.add))
                chain(dve.tensor_scalar(tmp, ps[:, :], -1.0, None, ALU.mult))
                chain(dve.scalar_tensor_tensor(out=tmp, in0=ps[:, :], scalar=0.25, in1=tmp,
                                               op0=ALU.max, op1=ALU.max))
                dve.sem_inc(free(f"mod{r}"), 1)
                chain(dve.tensor_tensor(dst[:], dst[:], tmp, ALU.mult))

            def mod_cols(name, i, n_ready):
                wait_job(dve, name)
                chain(dve.tensor_copy(mcol[:, i, :], psum(name)[:, 0:KH]))
                chain(dve.tensor_scalar(mcol[:, i + 1, :], psum(name)[:, KH:2 * KH], 1.0, None, ALU.add))
                dve.sem_inc(free(name), 1)
                dve.sem_inc(mcol_ready, 1)

            wait_load(dve, "c")
            chain(dve.tensor_scalar(ccol[:, 2, :], ccol[:, 0, :], 0.5, None, ALU.mult))
            dve.wait_ge(c_tanh, 1)
            chain(dve.scalar_tensor_tensor(out=ccol[:, 2, :], in0=ccol[:, 1, :], scalar=1.0, in1=ccol[:, 2, :],
                                           op0=ALU.add, op1=ALU.mult))
            dve.tensor_copy(cbc, ccol[:, 2, :].rearrange("p (k o) -> p k o", o=1).broadcast_to([P, KH, P])
                            ).then_inc(c_ready, 1)
            wait_load(dve, "consts")
            dve.tensor_scalar(dcols[:, CW:DP], dcols[:, CW:DP], 0.5, None, ALU.mult).then_inc(c_ready, 1)
            dve.wait_ge(c_ready, 2)
            dve.wait_ge(consts_set, 1)
            mod_cols("modA", 0, 1)
            for c, slot in slots():
                g = c * NS + slot
                if 0 < g <= UNITS:
                    if slot == 0 and g < UNITS:
                        keep_last(g - 1)
                        dve.wait_ge(carried, NS * c)
                        dve.wait_ge(first_exp, c)
                        chain(dve.tensor_tensor(inj[c % 2][:], inj[c % 2][:], carry[:], ALU.mult))
                if in_back(c):
                    back(c - 1, slot)
                if in_front(c):
                    front(c + 1, slot)
                if c == -1 and slot == 8:
                    gate_row(GA, gar)
                    gate_row(GB, gbr)
                    mod_cols("modB", 2, 2)
                if 0 <= g < UNITS:
                    scan(g)
                if 0 < g <= UNITS:
                    if not (slot == 0 and g < UNITS):
                        keep_last(g - 1)
                    add_states(g - 1)
            chain(dve.tensor_copy(idx[:], topi[:, :, 0:TOPK]))
            dve.tensor_tensor(hot[:].rearrange("p t k e -> p (t k) e"),
                              idx[:].rearrange("p t (k o) -> p (t k) o", o=1).broadcast_to([P, NT * TOPK, NE]),
                              iota[:, None, :].broadcast_to([P, NT * TOPK, NE]), ALU.is_equal).then_inc(hot_ready, 1)
            dve.tensor_tensor(ediff[:, :, 0:1], topv[:, :, 1:2], topv[:, :, 0:1], ALU.subtract).then_inc(diff_ready, 1)
            dve.wait_ge(ediff_ready, 1)
            chain(dve.tensor_scalar(prob[:, :, 0:1], ediff[:, :, 1:2], 1.0, None, ALU.add))
            chain(dve.reciprocal(prob[:, :, 0:1], prob[:, :, 0:1]))
            chain(dve.tensor_tensor(prob[:, :, 1:2], prob[:, :, 0:1], ediff[:, :, 1:2], ALU.mult))
            dve.wait_ge(hot_ready, 1)
            chain(dve.tensor_tensor(hotw.rearrange("p t k e -> p (t k) e"),
                                    hot[:].rearrange("p t k e -> p (t k) e"),
                                    prob[:].rearrange("p t (k o) -> p (t k) o", o=1).broadcast_to([P, NT * TOPK, NE]),
                                    ALU.mult))
            wait_job(dve, "count")
            chain(dve.tensor_scalar(allowed[:].rearrange("p k e -> p (k e)"), psum("count")[:, 0:TOPK * NE],
                                    float(CAP), None, ALU.is_le))
            dve.sem_inc(free("count"), 1)
            chain(dve.tensor_tensor(hotw.rearrange("p t k e -> p t (k e)"),
                                    hotw.rearrange("p t k e -> p t (k e)"),
                                    allowed[:].rearrange("p k e -> p (k e)")[:, None, :].broadcast_to([P, NT, TOPK * NE]),
                                    ALU.mult))
            chain(dve.tensor_tensor(wexp, hotw[:, :, 0, :], hotw[:, :, 1, :], ALU.add))
            dve.wait_ge(lt_ready, CHUNKS)
            dve.scalar_tensor_tensor(
                out=lw.rearrange("p t (e r) -> p (t e) r", e=NE),
                in0=lt[:].rearrange("p t (e r) -> p (t e) r", e=NE), scalar=ALPHA,
                in1=wexp.rearrange("p t (e o) -> p (t e) o", o=1).broadcast_to([P, NT * NE, ER]),
                op0=ALU.mult, op1=ALU.mult).then_inc(lw_ready, 1)
            dve.wait_ge(x2_back, 16)
            for t in range(NT):
                name = f"lo{t}"
                wait_job(dve, name)
                if t >= 4:
                    dve.wait_ge(out_stored[t % 4], 16 * (t // 4))
                chain(dve.tensor_tensor(fin[:, t % 4, :], gbr[:], psum(name)[:, :], ALU.mult))
                dve.sem_inc(free(name), 1)
                dve.tensor_tensor(fin[:, t % 4, :], fin[:, t % 4, :], x2r[:, t, :], ALU.add).then_inc(fin_ready, 1)


def kernel(**inputs):
    import numpy as np
    import concourse.bacc as bacc
    from concourse.bass_utils import run_bass_kernel_spmd

    a = {k: np.asarray(v) for k, v in inputs.items()}

    def tiles(m):
        return np.ascontiguousarray(m.reshape(-1, P, m.shape[1]).transpose(1, 0, 2))

    def cols(v):
        return v.reshape(KD, P, -1).transpose(1, 0, 2).reshape(P, -1)

    w_in = a["L0_attn_W_in"].T
    a_cols = a["L0_attn_A"].reshape(KD, P, NS).transpose(1, 2, 0).reshape(P, -1)
    arrays = {
        "x": a["L0_attn_hidden_states"].reshape(T, H),
        "w_in_u": tiles(w_in[:, :D]),
        "w_in_g": tiles(w_in[:, D:]),
        "dcols": np.concatenate([cols(a["L0_attn_conv_w"]), cols(a["L0_attn_conv_b"]),
                                 cols(a["L0_attn_D_param"]), a_cols], axis=1),
        "w_x": tiles(a["L0_attn_Wx"].T),
        "w_dt": np.concatenate([a["L0_attn_Wdt"].T, a["L0_attn_dt_bias"][None, :]], axis=0),
        "w_out": tiles(a["L0_attn_W_out"].T),
        "w_ffn": tiles(a["L0_ffn_weight"].T),
        "lora_a": tiles(a["L0_ffn_lora_A"].transpose(1, 0, 2).reshape(H, NE * ER)),
        "lora_b": a["L0_ffn_lora_B"].reshape(NE * ER, H),
        "gw1": tiles(a["L0_ffn_gw1"].T),
        "gw2": a["L0_ffn_gw2"].T,
        "rows": np.concatenate([a["L0_attn_dt_ln_w"], a["L0_attn_b_ln_w"], a["L0_attn_c_ln_w"], a["L0_ffn_gb1"],
                                a["L0_ffn_ln_gamma"], a["L0_ffn_ln_beta"], a["L0_ffn_gb2"]])[None, :],
        "c": a["L0_c"].reshape(KH, P).T,
        "w_mod": tiles(a["L0_wmod"]),
        "ident": np.eye(P, dtype=np.float32),
        "iota": np.tile(np.arange(NE, dtype=np.float32), (P, 1)),
    }
    nc = bacc.Bacc("TRN2", target_bir_lowering=False, num_devices=1)
    named, args = {}, []
    for name, v in arrays.items():
        v = np.ascontiguousarray(v)
        named[f"in_{name}"] = v
        args.append(nc.dram_tensor(f"in_{name}", v.shape, mybir.dt.from_np(v.dtype), kind="ExternalInput").ap())
    args.append(nc.dram_tensor("out", (T, H), F32, kind="ExternalOutput").ap())
    adaln_block(nc, *args)
    r = run_bass_kernel_spmd(nc, [named], core_ids=[0])
    return r.results[0]["out"].reshape(1, T, H)
```

```python
from contextlib import ExitStack

import concourse.bass as bass
from concourse import mybir

F32 = mybir.dt.float32
U32 = mybir.dt.uint32
ALU = mybir.AluOpType
ACT = mybir.ActivationFunctionType
AX_X = mybir.AxisListType.X

P = 128
T = 1024
H = 512
D = 1024
NS = 16
R = 32
KW = 4
NE, TOPK, ER, GH = 8, 2, 16, 32
CAP = int(3.0 * T / NE)
ALPHA = 1.0 / ER
RMS_EPS, LN_EPS = 1e-6, 1e-5

TC = 256
CHUNKS = T // TC
TT = TC // P
NT = T // P
KH = H // P
KD = D // P
PAIRS = KD // 2
UNITS = CHUNKS * NS
SLOTS = NS
SIDE = 4
N_DRIVE, N_DECAY, N_BREP = 3, 2, 2
NB = 2
XW = R + 2 * NS
CW, CB, DP, AC = 0, KD * KW, KD * KW + KD, KD * KW + 2 * KD
DCOLS = AC + NS * KD
R_LN, R_GB1, R_GAM, R_BET, R_GB2 = 0, XW, XW + GH, XW + 2 * GH, XW + 3 * GH
ROWS = R_GB2 + NE
SA, CA, GA, SB, CBM, GB = range(6)


TENSOR_STAGES = {
    1: ["b:y", "b:g0"], 2: ["b:g1", "b:g2"], 3: ["b:g3", "f:lnT"], 4: ["f:u0", "f:u1"], 5: ["f:u2", "b:oa0"],
    6: ["f:u3", "b:ob0"], 7: ["b:oa1", "b:ob1"], 9: ["f:xp"], 10: ["f:xpT", "b:l2T"], 11: ["b:gh", "b:m0"],
    12: ["f:dbT", "b:m1"], 13: ["f:dt"], 14: ["b:la", "b:ghT"], 15: ["b:gt"],
    (CHUNKS, 11): ["b:gh", "b:la"], (CHUNKS, 12): ["b:ghT"], (CHUNKS, 13): ["b:gt"], (CHUNKS, 14): ["b:m0", "b:m1"],
    (CHUNKS, 15): []}
SCALAR_STAGES = {
    2: ["b:g0"], 3: ["b:g1", "b:g2", "f:lnT"], 4: ["b:g3", "f:u0", "f:u1"], 5: ["f:u2"], 6: ["f:u3"],
    8: ["f:tanh"], 9: ["f:xp"], 10: ["b:l2T"], 12: ["f:dbT"], 13: ["f:log"], 14: ["b:la", "b:ghT"], 15: ["f:first"]}
VECTOR_STAGES = {
    0: ["f:stats"], 1: ["f:norm", "b:skip"], 2: ["b:z0"], 3: ["b:z1", "b:z2"], 4: ["b:z3"],
    5: ["f:conv0", "f:conv1"], 6: ["f:conv2"], 7: ["f:conv3", "b:o0"], 8: ["b:o1", "b:stats", "f:silu"],
    9: ["b:norm"], 10: ["f:rms"], 11: ["f:rmsn", "b:gate1"], 12: ["b:m0"], 13: ["b:gate2", "b:m1"],
    14: ["f:delta"], 15: ["b:top"],
    (CHUNKS, 12): ["b:gate2"], (CHUNKS, 13): ["b:top"], (CHUNKS, 15): []}
POOL_STAGES = {0: ["f:rstd"], 8: ["b:rstd"], 10: ["f:rms"], 11: ["b:rgate"]}
SCALAR_STAGES_FIRST = (2, 3, 4, 12, 13)
JOBS_OF = {"y": ["y0", "y1", "y2", "y3"], "lnT": ["lnT0", "lnT1"], "l2T": ["l2T0", "l2T1"], "oa0": ["o0"], "ob0": [],
           "oa1": ["o1"], "ob1": [], "dt": ["dt0", "dt1", "dt2", "dt3"]}


SETUP_JOBS = {3: ["modA"], 10: ["modga", "modB"], 11: ["modgb"]}
EARLY = {"u0": "g0", "u1": "g1", "u2": "g2", "u3": "g3", "conv0": "e0", "conv1": "e1", "conv2": "e2", "conv3": "e3"}


def chunk_stages(table, c, slot):
    for stage in table.get((CHUNKS, slot) if c == CHUNKS and (CHUNKS, slot) in table else slot, []):
        part, stage = stage.split(":")
        if part == "f" and c + 1 < CHUNKS:
            yield c + 1, stage
        if part == "f" and c + 1 == CHUNKS and stage in EARLY:
            yield c, EARLY[stage]
        if part == "b" and c >= 1 and not (c == CHUNKS and stage in ("g0", "g1", "g2", "g3")):
            yield c - 1, stage


def plan_jobs():
    names = []
    for c in range(-1, CHUNKS + 1):
        for slot in range(SLOTS):
            names += SETUP_JOBS.get(slot, []) if c == -1 else []
            for of, stage in chunk_stages(TENSOR_STAGES, c, slot):
                names += [f"{j}.{of}" for j in JOBS_OF.get(stage, [stage])]
    names += ["count"] + [f"lwT{j}" for j in range(2)] + [f"lo{t}" for t in range(NT)]
    return {n: (i % SIDE, i // SIDE + 1) for i, n in enumerate(names)}


def adaln_block(nc, x, w_in_u, w_in_g, dcols_d, w_x, w_dt, w_out, w_ffn, lora_a, lora_b, gw1, gw2,
                rows_d, c_d, w_mod, ident_d, iota_d, out):
    jobs = plan_jobs()
    b_scratch = nc.dram_tensor("b_scratch", (CHUNKS, NS, TC), F32, kind="Internal").ap()
    x2_scratch = nc.dram_tensor("x2_scratch", (T, H), F32, kind="Internal").ap()

    with ExitStack() as ctx:
        def sb(name, shape, dt=F32):
            return ctx.enter_context(nc.sbuf_tensor(name, shape, dt))

        def sem(name):
            return ctx.enter_context(nc.semaphore(name))

        wu = sb("wu", [P, KH, D])
        wg = sb("wg", [P, KH, D])
        wo = sb("wo", [P, KD, H])
        wf = sb("wf", [P, KH, H])
        wla = sb("wla", [P, KH, NE * ER])
        wlb = sb("wlb", [P, H])
        wx = sb("wx", [P, KD, XW])
        wdt = sb("wdt", [R + 1, D])
        wg1 = sb("wg1", [P, KH, GH])
        wg2 = sb("wg2", [GH, NE])
        dcols = sb("dcols", [P, DCOLS])
        rows = sb("rows", [P, ROWS])
        ident = sb("ident", [P, P])
        iota = sb("iota", [P, NE])
        ones = sb("ones", [P, P])
        ccol = sb("ccol", [P, 3, KH])
        mcol = sb("mcol", [P, 4, KH])
        gar = sb("gar", [P, H])
        gbr = sb("gbr", [P, H])
        big = sb("big", [P, 6, KD * TC])
        wmod = big[:, :, :].rearrange("p a b -> p (a b)").rearrange("p (k n) -> p k n", k=KH)
        drive = [big[:, i, :].rearrange("p (d t) -> p d t", d=KD) for i in range(N_DRIVE)]
        acc = big[:, 3, :].rearrange("p (t d) -> p t d", t=TT)
        decay = [big[:, 4 + i, :].rearrange("p (d t) -> p d t", d=KD) for i in range(N_DECAY)]
        x2r = big[:, 0:2, :].rearrange("p a b -> p (a b)").rearrange("p (t h) -> p t h", t=NT)[:, 0:NT - TT, :]
        lwT = big[:, 4, 0:NT * P].rearrange("p (t n) -> p t n", t=NT)
        lw = big[:, 5, 0:NT * P].rearrange("p (t n) -> p t n", t=NT)
        fin = big[:, 3, :].rearrange("p (b h) -> p b h", h=H)
        xin = sb("xin", [P, TT, H])
        xn = sb("xn", [P, TT, H])
        hT = [sb(f"hT{i}", [P, KH, TC]) for i in range(2)]
        upre = [sb(f"upre{i}", [P, 2, KW - 1 + TC]) for i in range(2)]
        halo = sb("halo", [P, KD, KW - 1])
        xh = sb("xh", [P, KD, TC])
        u = [sb(f"u{i}", [P, KD, TC]) for i in range(2)]
        ssT = upre[0][0:XW, 0, 0:TC]
        bT = upre[1][0:R + NS, 0, 0:TC]
        ghT = upre[1][0:GH, 1, 0:TC]
        ss = sb("ss", [P, TT, XW])
        sq = sb("sq", [P, TT, XW])
        ssn = [sb(f"ssn{i}", [P, TT, XW]) for i in range(2)]
        rinv = sb("rinv", [P, TT, 3])
        dtT = sb("dtT", [R + 1, TC])
        delta = sb("delta", [P, KD, TC])
        du = sb("du", [P, KD, TC])
        brep = [sb(f"brep{i}", [P, NB, TC]) for i in range(N_BREP)]
        carry = sb("carry", [P, NS, KD])
        inj = [sb(f"inj{i}", [P, NS, KD]) for i in range(2)]
        stat = sb("stat", [P, TT, 6])
        mv = sb("mv", [P, TT, 2])
        rstd = sb("rstd", [P, TT, 1])
        mhalf = sb("mhalf", [P, 8])
        xres = sb("xres", [P, TT, H])
        gth = [sb(f"gth{i}", [P, 2, TC]) for i in range(2)]
        h2T = sb("h2T", [P, KH, TC])
        tmp = gth[0][:].rearrange("p i t -> p (i t)")
        stat2 = sb("stat2", [P, TT, 6])
        mv2 = sb("mv2", [P, TT, 2])
        rstd2 = sb("rstd2", [P, TT, 1])
        gh = sb("gh", [P, TT, GH])
        gates = sb("gates", [P, TT, NE])
        lt = sb("lt", [P, NT, NE * ER])
        cbc = lt[:, 0:KH, :]
        topv = sb("topv", [P, NT, 8])
        topi = sb("topi", [P, NT, 8], U32)
        idx = sb("idx", [P, NT, TOPK])
        hot = sb("hot", [P, NT, TOPK, NE])
        hotw = big[:, 3, 0:NT * TOPK * NE].rearrange("p (t k e) -> p t k e", k=TOPK, e=NE)
        allowed = sb("allowed", [P, TOPK, NE])
        prob = sb("prob", [P, NT, TOPK])
        ediff = sb("ediff", [P, NT, 2])
        wexp = big[:, 2, 0:NT * NE].rearrange("p (t e) -> p t e", e=NE)

        side = [ctx.enter_context(nc.psum_tensor(f"side{i}", [P, 512], F32)) for i in range(SIDE)]
        stT = [ctx.enter_context(nc.psum_tensor(f"stT{i}", [P, KD * P], F32)) for i in range(2)]

        bank_ready = [sem(f"bank_ready{i}") for i in range(SIDE)]
        bank_free = [sem(f"bank_free{i}") for i in range(SIDE)]
        loads = ["c", "consts", "wm0", "wm1", "wm2", "wu", "wx", "wg", "wo", "wf", "small", "lora"]
        loaded = {n: sem(f"ld_{n}") for n in loads}
        n_load = {}
        xin_loaded, xres_loaded = sem("xin_loaded"), sem("xres_loaded")
        x2_stored, x2_back = sem("x2_stored"), sem("x2_back")
        out_stored = [sem(f"out_stored{i}") for i in range(4)]
        b_stored = sem("b_stored")
        brep_loaded = [sem(f"brep_loaded{i}") for i in range(N_BREP)]
        dve_chain, pool_chain, act_chain = sem("dve_chain"), sem("pool_chain"), sem("act_chain")
        consts_set, c_tanh, c_ready = sem("consts_set"), sem("c_tanh"), sem("c_ready")
        mcol_ready, gates_ready, scaled = sem("mcol_ready"), sem("gates_ready"), sem("scaled")
        var_ready, rstd_ready, xn_ready, xin_used = sem("var_ready"), sem("rstd_ready"), sem("xn_ready"), sem("xin_used")
        hT_ready, taps_ready, conv_done, halo_saved = sem("hT_ready"), sem("taps_ready"), sem("conv_done"), sem("halo_saved")
        tanh_ready, u_ready = sem("tanh_ready"), sem("u_ready")
        ssT_ready, ms_ready, rinv_ready, ssn_ready = sem("ssT_ready"), sem("ms_ready"), sem("rinv_ready"), sem("ssn_ready")
        bT_ready, dtT_ready = sem("bT_ready"), sem("dtT_ready")
        log_ready, delta_ready, du_ready = sem("log_ready"), sem("delta_ready"), sem("du_ready")
        first_ready, first_exp = sem("first_ready"), sem("first_exp")
        decay_ready, drive_ready, scanned = sem("decay_ready"), sem("drive_ready"), sem("scanned")
        turned, added, carried, acc_read = sem("turned"), sem("added"), sem("carried"), sem("acc_read")
        gth_ready, z_ready, early_ready = sem("gth_ready"), sem("z_ready"), sem("early_ready")
        x2_ready = sem("x2_ready")
        h2T_ready, x2m_ready = sem("h2T_ready"), sem("x2m_ready")
        gvar_ready, grstd_ready, gh_ready = sem("gvar_ready"), sem("grstd_ready"), sem("gh_ready")
        ghT_ready = sem("ghT_ready")
        lt_ready, hot_ready, diff_ready, ediff_ready = sem("lt_ready"), sem("hot_ready"), sem("diff_ready"), sem("ediff_ready")
        lw_ready, lwT_ready, fin_ready = sem("lw_ready"), sem("lwT_ready"), sem("fin_ready")

        def psum(name):
            return side[jobs[name][0]]

        def wait_job(eng, name):
            bank, nth = jobs[name]
            eng.wait_ge(bank_ready[bank], nth)

        def free(name):
            return bank_free[jobs[name][0]]

        class Chain:

            def __init__(self, eng, s):
                self.eng, self.s, self.n = eng, s, 0

            def __call__(self, ins):
                self.n += 1
                ins.then_inc(self.s, 1)
                self.eng.wait_ge(self.s, self.n)

        def wait_load(eng, name):
            eng.wait_ge(loaded[name], 16 * n_load[name])

        def xn_front(c):
            return TT * (c + 1 + max(0, c - 2))

        def xn_back(c):
            return TT * (min(c + 3, CHUNKS) + c + 1)

        def slots():
            for c in range(-1, CHUNKS + 1):
                for slot in range(SLOTS):
                    yield c, slot

        def stages(table, c, slot, front, back):
            for of, stage in chunk_stages(table, c, slot):
                (front if of == c + 1 else back)(of, stage)

        def wait_mod_done(eng):
            for name in ("modA", "modga", "modB", "modgb"):
                wait_job(eng, name)

        block = ctx.enter_context(nc.Block())

        @block.sync
        def _(sp):
            def load(group, dst, src):
                n_load[group] = n_load.get(group, 0) + 1
                sp.dma_start(dst, src).then_inc(loaded[group], 16)

            load("c", ccol[:, 0, :], c_d)
            xt = x.rearrange("(c t p) h -> c p t h", p=P, t=TT)
            sp.dma_start(xin[:], xt[0]).then_inc(xin_loaded, 16)
            load("consts", ident[:], ident_d)
            load("wm0", wmod[:, :, 0:1024], w_mod[:, :, 0:1024])
            load("consts", iota[:], iota_d)
            load("consts", dcols[:], dcols_d)
            load("consts", rows[:], rows_d.broadcast_to([P, ROWS]))
            load("wu", wu[:], w_in_u)
            load("wx", wx[:], w_x)
            load("wx", wdt[:], w_dt)
            load("wm1", wmod[:, :, 1024:2048], w_mod[:, :, 1024:2048])
            load("wm2", wmod[:, :, 2048:3072], w_mod[:, :, 2048:3072])
            load("wo", wo[:], w_out)
            load("wf", wf[:], w_ffn)
            load("lora", wla[:], lora_a)
            load("lora", wlb[:], lora_b)
            load("small", wg1[:], gw1)
            load("small", wg2[:], gw2)
            load("wg", wg[:], w_in_g)

            for c, slot in slots():
                if c + 2 < CHUNKS and slot == 4:
                    sp.wait_ge(xin_used, c + 2)
                    sp.dma_start(xin[:], xt[c + 2]).then_inc(xin_loaded, 16)
                if c >= 1 and slot == 0:
                    if c >= 2:
                        sp.wait_ge(x2_stored, 16 * (c - 1))
                    sp.dma_start(xres[:], xt[c - 1]).then_inc(xres_loaded, 16)
                if c + 1 < CHUNKS and slot == 13:
                    sp.wait_ge(bT_ready, c + 2)
                    sp.dma_start(b_scratch[c + 1], bT[R:R + NS, :]).then_inc(b_stored, 16)
                g = c * NS + slot + 2
                if g % NB == 0 and 0 <= g < UNITS:
                    j = g // NB
                    if g % NS == 0:
                        sp.wait_ge(b_stored, 16 * (g // NS + 1))
                    if j >= N_BREP:
                        sp.wait_ge(drive_ready, NB * (j - N_BREP) + NB)
                    cc, n = g // NS, g % NS
                    src = b_scratch[cc:cc + 1, n:n + NB, :].broadcast_to([P, NB, TC])
                    sp.dma_start(brep[j % N_BREP][:], src).then_inc(brep_loaded[j % N_BREP], 16)
                if 1 <= c < CHUNKS and slot == 14:
                    sp.wait_ge(x2m_ready, TT * c)
                    sp.dma_start(x2_scratch.rearrange("(c t p) h -> c p t h", p=P, t=TT)[c - 1],
                                 xres[:]).then_inc(x2_stored, 16)
            sp.wait_ge(x2_stored, 16 * (CHUNKS - 1))
            sp.wait_ge(turned, TT * UNITS)
            sp.wait_ge(carried, UNITS - NS)
            sp.dma_start(x2r, x2_scratch[0:(NT - TT) * P, :].rearrange("(t p) h -> p t h", p=P)
                         ).then_inc(x2_back, 16)
            for t in range(NT):
                sp.wait_ge(fin_ready, t + 1)
                sp.dma_start(out[t * P:(t + 1) * P, :], fin[:, t % 4, :]).then_inc(out_stored[t % 4], 16)
            for i in range(4):
                sp.wait_ge(out_stored[i], 16 * NT // 4)

        @block.tensor
        def _(pe):
            def begin(name):
                bank, nth = jobs[name]
                if nth > 1:
                    pe.wait_ge(bank_free[bank], nth - 1)
                return side[bank]

            def end(name, ins):
                ins.then_inc(bank_ready[jobs[name][0]], 1)

            def mod_row(name, r):
                ps = begin(name)
                wait_load(pe, f"wm{r // 2}")
                for k in range(KH):
                    last = pe.matmul(ps[:, :], cbc[:, k, :], wmod[:, k, r * H:(r + 1) * H],
                                     start=(k == 0), stop=(k == KH - 1))
                end(name, last)

            def mod_cols(name, rows_):
                ps = begin(name)
                for i, r in enumerate(rows_):
                    wait_load(pe, f"wm{r // 2}")
                    for m in range(KH):
                        for k in range(KH):
                            f = r * H + m * P
                            last = pe.matmul(ps[:, i * KH + m:i * KH + m + 1], wmod[:, k, f:f + P],
                                             ccol[:, 2, k:k + 1], start=(k == 0), stop=(k == KH - 1))
                end(name, last)

            def turn_tokens(job, src):
                for j in range(2):
                    ps = begin(job(j))
                    for k in range(2):
                        for t in range(TT):
                            f = (2 * j + k) * P
                            last = pe.transpose(ps[:, k * TC + t * P:k * TC + (t + 1) * P],
                                                src[:, t, f:f + P], ident[:])
                    end(job(j), last)

            def project_pair(name, weights, q, rhs):
                ps = begin(name)
                for i in range(2):
                    d0 = (2 * q + i) * P
                    for k in range(KH):
                        last = pe.matmul(ps[:, i * TC:(i + 1) * TC], weights[:, k, d0:d0 + P], rhs[:, k, :],
                                         start=(k == 0), stop=(k == KH - 1))
                end(name, last)

            def front(c, stage):
                if stage == "lnT":
                    pe.wait_ge(xn_ready, xn_front(c))
                    turn_tokens(lambda j: f"lnT{j}.{c}", xn)
                if stage[0] == "u":
                    pe.wait_ge(hT_ready, KH * (c + 1))
                    project_pair(f"{stage}.{c}", wu, int(stage[1]), hT[c % 2])
                if stage == "xp":
                    ps = begin(f"xp.{c}")
                    pe.wait_ge(u_ready, 2 * (c + 1))
                    for k in range(KD):
                        last = pe.matmul(ps[0:XW, 0:TC], wx[:, k, :], u[c % 2][:, k, :],
                                         start=(k == 0), stop=(k == KD - 1))
                    end(f"xp.{c}", last)
                if stage == "xpT":
                    ps = begin(f"xpT.{c}")
                    pe.wait_ge(ssT_ready, c + 1)
                    for t in range(TT):
                        last = pe.transpose(ps[:, t * XW:(t + 1) * XW], ssT[:, t * P:(t + 1) * P],
                                            ident[0:XW, 0:XW])
                    end(f"xpT.{c}", last)
                if stage == "dbT":
                    ps = begin(f"dbT.{c}")
                    pe.wait_ge(ssn_ready, c + 1)
                    for t in range(TT):
                        last = pe.transpose(ps[0:R + NS, t * P:(t + 1) * P], ssn[c % 2][:, t, 0:R + NS], ident[:])
                    end(f"dbT.{c}", last)
                if stage == "dt":
                    pe.wait_ge(dtT_ready, c + 1)
                    for q in range(PAIRS):
                        ps = begin(f"dt{q}.{c}")
                        for i in range(2):
                            d0 = (2 * q + i) * P
                            last = pe.matmul(ps[:, i * TC:(i + 1) * TC], wdt[:, d0:d0 + P], dtT[:, :],
                                             start=True, stop=True)
                        end(f"dt{q}.{c}", last)

            def back(c, stage):
                if stage == "y":
                    pe.wait_ge(added, TT * NS * (c + 1))
                    for q in range(PAIRS):
                        ps = begin(f"y{q}.{c}")
                        for i in range(2):
                            for t in range(TT):
                                d0 = (2 * q + i) * P
                                last = pe.transpose(ps[:, i * TC + t * P:i * TC + (t + 1) * P],
                                                    acc[:, t, d0:d0 + P], ident[:])
                        end(f"y{q}.{c}", last)
                if stage in ("g0", "g1", "g2", "g3"):
                    wait_load(pe, "wg")
                    project_pair(f"{stage}.{c}", wg, int(stage[1]), hT[c % 2])
                if stage[0] == "o":
                    t, first = int(stage[2]), stage[1] == "a"
                    ps = begin(f"o{t}.{c}") if first else psum(f"o{t}.{c}")
                    pe.wait_ge(scaled, 3)
                    pe.wait_ge(z_ready, PAIRS * (c + 1))
                    for k in range(KD)[:KD // 2] if first else range(KD)[KD // 2:]:
                        last = pe.matmul(ps[:, :], u[c % 2][:, k, t * P:(t + 1) * P], wo[:, k, :],
                                         start=(k == 0), stop=(k == KD - 1))
                    if not first:
                        end(f"o{t}.{c}", last)
                if stage == "l2T":
                    pe.wait_ge(xn_ready, xn_back(c))
                    turn_tokens(lambda j: f"l2T{j}.{c}", xn)
                if stage == "gh":
                    ps = begin(f"gh.{c}")
                    pe.wait_ge(h2T_ready, KH * (c + 1))
                    wait_load(pe, "small")
                    wait_load(pe, "lora")
                    for t in range(TT):
                        for k in range(KH):
                            last = pe.matmul(ps[:, t * GH:(t + 1) * GH], h2T[:, k, t * P:(t + 1) * P],
                                             wg1[:, k, :], start=(k == 0), stop=(k == KH - 1))
                    end(f"gh.{c}", last)
                if stage == "la":
                    ps = begin(f"la.{c}")
                    for t in range(TT):
                        for k in range(KH):
                            last = pe.matmul(ps[:, t * P:(t + 1) * P], h2T[:, k, t * P:(t + 1) * P],
                                             wla[:, k, :], start=(k == 0), stop=(k == KH - 1))
                    end(f"la.{c}", last)
                if stage in ("m0", "m1"):
                    t = int(stage[1])
                    ps = begin(f"m{t}.{c}")
                    for k in range(KH):
                        last = pe.matmul(ps[:, :], h2T[:, k, t * P:(t + 1) * P], wf[:, k, :],
                                         start=(k == 0), stop=(k == KH - 1))
                    end(f"m{t}.{c}", last)
                if stage == "ghT":
                    ps = begin(f"ghT.{c}")
                    pe.wait_ge(gh_ready, c + 1)
                    for t in range(TT):
                        last = pe.transpose(ps[0:GH, t * P:(t + 1) * P], gh[:, t, :], ident[:])
                    end(f"ghT.{c}", last)
                if stage == "gt":
                    ps = begin(f"gt.{c}")
                    pe.wait_ge(ghT_ready, c + 1)
                    for t in range(TT):
                        last = pe.matmul(ps[:, t * NE:(t + 1) * NE], ghT[:, t * P:(t + 1) * P], wg2[:, :],
                                         start=True, stop=True)
                    end(f"gt.{c}", last)

            pe.wait_ge(consts_set, 1)
            wait_load(pe, "consts")
            pe.wait_ge(c_ready, 1)
            for c, slot in slots():
                if c == -1 and slot == 3:
                    mod_cols("modA", (SA, CA))
                if c == -1 and slot == 4:
                    wait_load(pe, "wu")
                if c == -1 and slot == 9:
                    wait_load(pe, "wx")
                if c == -1 and slot == 10:
                    mod_row("modga", GA)
                    mod_cols("modB", (SB, CBM))
                if c == -1 and slot == 11:
                    mod_row("modgb", GB)
                stages(TENSOR_STAGES, c, slot, front, back)
                if 0 <= c < CHUNKS:
                    g = c * NS + slot
                    for t in range(TT):
                        k = TT * g + t
                        pe.wait_ge(scanned, g + 1)
                        if k >= 2:
                            pe.wait_ge(added, k - 1)
                        for d in range(KD):
                            last = pe.transpose(stT[k % 2][:, d * P:(d + 1) * P],
                                                drive[g % N_DRIVE][:, d, t * P:(t + 1) * P], ident[:])
                        last.then_inc(turned, 1)
            ps = begin("count")
            pe.wait_ge(hot_ready, 1)
            for t in range(NT):
                last = pe.matmul(ps[:, 0:TOPK * NE], ones[:], hot[:, t, :, :].rearrange("p k e -> p (k e)"),
                                 start=(t == 0), stop=(t == NT - 1))
            end("count", last)
            pe.wait_ge(lw_ready, 1)
            for j in range(2):
                ps = begin(f"lwT{j}")
                for i in range(NT // 2):
                    last = pe.transpose(ps[:, i * P:(i + 1) * P], lw[:, j * NT // 2 + i, :], ident[:])
                end(f"lwT{j}", last)
            for t in range(NT):
                ps = begin(f"lo{t}")
                pe.wait_ge(lwT_ready, t // (NT // 2) + 1)
                end(f"lo{t}", pe.matmul(ps[:, :], lwT[:, t, :], wlb[:, :], start=True, stop=True))

        @block.scalar
        def _(act):
            def evacuate_norm(job, dst, shift, ready):
                for j in range(2):
                    wait_job(act, job(j))
                    for i in range(2):
                        k = 2 * j + i
                        ins = act.activation(dst[:, k, :], psum(job(j))[:, i * TC:(i + 1) * TC], ACT.Identity,
                                             bias=mcol[:, shift, k:k + 1], scale=mcol[:, shift + 1, k:k + 1])
                        ins.then_inc(ready, 1)
                    act.wait_ge(ready, evacuate_norm.n + 2 * j + 2)
                    act.sem_inc(free(job(j)), 1)

            def front(c, stage):
                if stage == "lnT":
                    if c == 0:
                        act.wait_ge(mcol_ready, 1)
                    evacuate_norm.n = KH * c
                    evacuate_norm(lambda j: f"lnT{j}.{c}", hT[c % 2], 0, hT_ready)
                if stage[0] == "u":
                    q = int(stage[1])
                    name = f"u{q}.{c}"
                    if c == 0 and q == 0:
                        act.wait_ge(c_ready, 2)
                    wait_job(act, name)
                    if c >= 1 and q == 1:
                        act.wait_ge(b_stored, 16 * c)
                    if 4 * c + q >= 2:
                        act.wait_ge(conv_done, 4 * c + q - 1)
                        act.wait_ge(halo_saved, 4 * c + q - 1)
                    act.activation(upre[q % 2][:, :, KW - 1:], psum(name)[:, :].rearrange("p (i t) -> p i t", i=2),
                                   ACT.Copy).then_inc(taps_ready, 1)
                    for i in range(2):
                        d = 2 * q + i
                        ins = act.activation(xh[:, d, :], psum(name)[:, i * TC:(i + 1) * TC], ACT.Identity,
                                             bias=dcols[:, CB + d:CB + d + 1],
                                             scale=dcols[:, CW + d * KW + KW - 1:CW + d * KW + KW])
                        ins.then_inc(taps_ready, 1)
                    act.wait_ge(taps_ready, 3 * (4 * c + q + 1))
                    act.sem_inc(free(name), 1)
                if stage == "tanh":
                    act.wait_ge(conv_done, 4 * (c + 1))
                    if c >= 2:
                        wait_job(act, f"o1.{c - 2}")
                    for j in range(2):
                        act.activation(u[c % 2][:, 4 * j:4 * j + 4, :], xh[:, 4 * j:4 * j + 4, :],
                                       ACT.Tanh).then_inc(tanh_ready, 1)
                if stage == "xp":
                    wait_job(act, f"xp.{c}")
                    act.wait_ge(halo_saved, 4 * (c + 1))
                    act.activation(ssT[:, :], psum(f"xp.{c}")[0:XW, 0:TC], ACT.Copy).then_inc(ssT_ready, 1)
                    act.wait_ge(ssT_ready, c + 1)
                    act.sem_inc(free(f"xp.{c}"), 1)
                if stage == "dbT":
                    name = f"dbT.{c}"
                    wait_job(act, name)
                    if c >= 1:
                        act.wait_ge(b_stored, 16 * c)
                    act.activation(dtT[0:R, :], psum(name)[0:R, 0:TC], ACT.Copy).then_inc(dtT_ready, 1)
                    act.activation(bT[R:R + NS, :], psum(name)[R:R + NS, 0:TC], ACT.Copy).then_inc(bT_ready, 1)
                    act.wait_ge(dtT_ready, c + 1)
                    act.wait_ge(bT_ready, c + 1)
                    act.sem_inc(free(name), 1)
                if stage == "log":
                    act.wait_ge(u_ready, 2 * (c + 1))
                    log = xh[:, :, :].rearrange("p d t -> p (d t)")
                    for q in range(PAIRS):
                        wait_job(act, f"dt{q}.{c}")
                        ins = act.activation(log[:, q * 512:(q + 1) * 512], psum(f"dt{q}.{c}")[:, :], ACT.Abs)
                        ins.then_inc(act_chain, 1)
                    act.wait_ge(act_chain, 5 * c + 4)
                    act.activation(log, log, ACT.Exp, scale=-1.0).then_inc(act_chain, 1)
                    act.wait_ge(act_chain, 5 * c + 5)
                    act.activation(log, log, ACT.Ln, bias=1.0).then_inc(log_ready, 1)
                if stage == "first" and c >= 1:
                    act.wait_ge(first_ready, c)
                    act.activation(inj[c % 2][:], inj[c % 2][:], ACT.Exp).then_inc(first_exp, 1)

            def back(c, stage):
                if stage in ("g0", "g1", "g2", "g3"):
                    q = int(stage[1])
                    wait_job(act, f"g{q}.{c}")
                    if c == CHUNKS - 1:
                        act.wait_ge(*((early_ready, q - 1) if q >= 2 else (z_ready, 4 * c)))
                    elif 4 * c + q >= 2:
                        act.wait_ge(z_ready, 4 * c + q - 1)
                    act.activation(gth[q % 2][:].rearrange("p i t -> p (i t)"), psum(f"g{q}.{c}")[:, :],
                                   ACT.Tanh, scale=0.5).then_inc(gth_ready, 1)
                if stage == "l2T":
                    if c == 0:
                        act.wait_ge(mcol_ready, 2)
                    evacuate_norm.n = KH * c
                    evacuate_norm(lambda j: f"l2T{j}.{c}", h2T, 2, h2T_ready)
                if stage == "la":
                    wait_job(act, f"la.{c}")
                    act.activation(lt[:, TT * c:TT * c + TT, :].rearrange("p t n -> p (t n)"),
                                   psum(f"la.{c}")[:, 0:TT * P], ACT.Copy).then_inc(lt_ready, 1)
                    act.wait_ge(lt_ready, c + 1)
                    act.sem_inc(free(f"la.{c}"), 1)
                if stage == "ghT":
                    wait_job(act, f"ghT.{c}")
                    act.activation(ghT[:, :], psum(f"ghT.{c}")[0:GH, 0:TC], ACT.Copy).then_inc(ghT_ready, 1)
                    act.wait_ge(ghT_ready, c + 1)
                    act.sem_inc(free(f"ghT.{c}"), 1)

            wait_load(act, "c")
            act.activation(ccol[:, 1, :], ccol[:, 0, :], ACT.Tanh, scale=0.5).then_inc(c_tanh, 1)

            for c, slot in slots():
                if slot in SCALAR_STAGES_FIRST:
                    stages(SCALAR_STAGES, c, slot, front, back)
                g = c * NS + slot + 2
                if 0 <= g < UNITS:
                    cc, n = g // NS, g % NS
                    if g == 0:
                        act.wait_ge(consts_set, 2)
                    if n == 0:
                        act.wait_ge(delta_ready, PAIRS * (cc + 1))
                    if g >= N_DECAY:
                        act.wait_ge(scanned, g - N_DECAY + 1)
                    for d in range(KD):
                        ins = act.activation(decay[g % N_DECAY][:, d, 1:], delta[:, d, 1:], ACT.Exp,
                                             scale=dcols[:, AC + n * KD + d:AC + n * KD + d + 1])
                    ins.then_inc(decay_ready, 1)
                if slot not in SCALAR_STAGES_FIRST:
                    stages(SCALAR_STAGES, c, slot, front, back)
            act.wait_ge(diff_ready, 1)
            act.activation(ediff[:, :, 1:2], ediff[:, :, 0:1], ACT.Exp).then_inc(ediff_ready, 1)
            act.wait_ge(decay_ready, UNITS)
            for j in range(2):
                wait_job(act, f"lwT{j}")
                half = NT // 2
                act.activation(lwT[:, j * half:(j + 1) * half, :].rearrange("p t n -> p (t n)"),
                               psum(f"lwT{j}")[:, :], ACT.Copy).then_inc(lwT_ready, 1)
                act.wait_ge(lwT_ready, j + 1)
                act.sem_inc(free(f"lwT{j}"), 1)

        @block.gpsimd
        def _(pool):
            chain = Chain(pool, pool_chain)
            pool.memset(mhalf[:], -0.5)
            chain(pool.memset(halo[:], 0.0))
            chain(pool.memset(dtT[R:R + 1, :], 1.0))
            chain(pool.memset(ones[:], 1.0))
            pool.sem_inc(consts_set, 1)

            def rsqrt(dst, src, n, done):
                pool.tensor_tensor(dst, src, mhalf[:, 0:n].rearrange("p (t o) -> p t o", t=TT),
                                   ALU.pow).then_inc(done, 1)

            n_var = 0

            def front(c, stage):
                nonlocal n_var
                if stage == "rstd":
                    n_var += 1
                    pool.wait_ge(var_ready, n_var)
                    rsqrt(rstd[:], rstd[:], TT, rstd_ready)
                if stage == "rms":
                    pool.wait_ge(ms_ready, c + 1)
                    rsqrt(rinv[:], rinv[:], 3 * TT, rinv_ready)

            def back(c, stage):
                nonlocal n_var
                if stage == "rstd":
                    n_var += 1
                    pool.wait_ge(var_ready, n_var)
                    rsqrt(rstd[:], rstd[:], TT, rstd_ready)
                if stage == "rgate":
                    pool.wait_ge(gvar_ready, c + 1)
                    rsqrt(rstd2[:], rstd2[:], TT, grstd_ready)

            for c, slot in slots():
                if c == -1 and slot == 12:
                    for gate, n, names, w in ((gar, 1, ("wo",), wo[:]), (gbr, 2, ("wf",), wf[:]), (gbr, 2, ("lora",), wlb[:, None, :])):
                        pool.wait_ge(gates_ready, n)
                        for name in names:
                            wait_load(pool, name)
                        k = w.shape[1]
                        pool.tensor_tensor(w, w, gate[:, None, :].broadcast_to([P, k, H]), ALU.mult).then_inc(scaled, 1)
                if 0 <= c < CHUNKS - 1 and slot == 14:
                    pool.wait_ge(drive_ready, NS * (c + 1))
                    pool.wait_ge(delta_ready, PAIRS * (c + 2))
                    pool.wait_ge(u_ready, 2 * (c + 2))
                    pool.tensor_tensor(du[:], delta[:], u[(c + 1) % 2][:], ALU.mult).then_inc(du_ready, 1)
                g = c * NS + slot + 2
                if 0 <= g < UNITS:
                    j = g // NB
                    if g == 0:
                        wait_mod_done(pool)
                        for i in range(N_DECAY):
                            chain(pool.memset(decay[i][:, :, 0:1], 0.0))
                        pool.sem_inc(consts_set, 1)
                    if g % NS == 0:
                        pool.wait_ge(du_ready, g // NS + 1)
                    pool.wait_ge(brep_loaded[j % N_BREP], 16 * (j // N_BREP + 1))
                    if g >= N_DRIVE:
                        pool.wait_ge(turned, TT * (g - N_DRIVE + 1))
                        if g - N_DRIVE < UNITS - NS:
                            pool.wait_ge(carried, g - N_DRIVE + 1)
                    pool.tensor_tensor(drive[g % N_DRIVE], du[:],
                                       brep[j % N_BREP][:, g % NB:g % NB + 1, :].broadcast_to([P, KD, TC]),
                                       ALU.mult).then_inc(drive_ready, 1)
                stages(POOL_STAGES, c, slot, front, back)

        @block.vector
        def _(dve):
            chain = Chain(dve, dve_chain)
            state = {"var": 0}

            def norm_stats(src):
                for t in range(TT):
                    ins = dve.bn_stats(stat[:, t, :], src[:, t, :])
                chain(ins)
                for t in range(TT):
                    ins = dve.bn_aggr(mv[:, t, :], stat[:, t, :])
                chain(ins)
                dve.tensor_scalar(rstd[:], mv[:, :, 1:2], LN_EPS, None, ALU.add).then_inc(var_ready, 1)
                state["var"] += 1

            def normalise(src):
                dve.wait_ge(rstd_ready, state["var"])
                for t in range(TT):
                    ins = dve.tensor_scalar(xn[:, t, :], src[:, t, :], mv[:, t, 0:1], rstd[:, t, :],
                                            ALU.subtract, ALU.mult)
                    ins.then_inc(xn_ready, 1)

            def front(c, stage):
                if stage == "stats":
                    dve.wait_ge(xin_loaded, 16 * (c + 1))
                    norm_stats(xin)
                if stage == "norm":
                    if c >= 1:
                        for j in range(2):
                            wait_job(dve, f"l2T{j}.{c - 3}" if c >= 3 else f"lnT{j}.{c - 1}")
                    normalise(xin)
                    dve.wait_ge(xn_ready, xn_front(c))
                    dve.sem_inc(xin_used, 1)
                if stage[:4] == "conv":
                    q = int(stage[4])
                    pre = upre[q % 2]
                    dve.wait_ge(taps_ready, 3 * (4 * c + q + 1))
                    chain(dve.tensor_copy(pre[:, :, 0:KW - 1], halo[:, 2 * q:2 * q + 2, :]))
                    for tap in range(KW - 1):
                        for i in range(2):
                            d = 2 * q + i
                            ins = dve.scalar_tensor_tensor(
                                out=xh[:, d, :], in0=pre[:, i, tap:tap + TC],
                                scalar=dcols[:, CW + d * KW + tap:CW + d * KW + tap + 1],
                                in1=xh[:, d, :], op0=ALU.mult, op1=ALU.add)
                            if tap == KW - 2:
                                break
                        if tap < KW - 2:
                            chain(ins)
                    d = 2 * q + 1
                    chain(ins)
                    dve.scalar_tensor_tensor(
                        out=xh[:, d, :], in0=pre[:, 1, KW - 2:KW - 2 + TC],
                        scalar=dcols[:, CW + d * KW + KW - 2:CW + d * KW + KW - 1],
                        in1=xh[:, d, :], op0=ALU.mult, op1=ALU.add).then_inc(conv_done, 1)
                    dve.tensor_copy(halo[:, 2 * q:2 * q + 2, :], pre[:, :, TC:TC + KW - 1]).then_inc(halo_saved, 1)
                if stage == "silu":
                    for j in range(2):
                        dve.wait_ge(tanh_ready, 2 * c + j + 1)
                        s = slice(4 * j, 4 * j + 4)
                        flat = lambda a: a[:, s, :].rearrange("p d t -> p (d t)")
                        dve.scalar_tensor_tensor(out=flat(u[c % 2]), in0=flat(u[c % 2]), scalar=1.0,
                                                 in1=flat(xh), op0=ALU.add, op1=ALU.mult).then_inc(u_ready, 1)
                if stage == "rms":
                    name = f"xpT.{c}"
                    wait_job(dve, name)
                    chain(dve.tensor_copy(ss[:].rearrange("p t n -> p (t n)"), psum(name)[:, 0:TT * XW]))
                    dve.sem_inc(free(name), 1)
                    chain(dve.tensor_tensor(sq[:], ss[:], ss[:], ALU.mult))
                    dve.tensor_reduce(rinv[:, :, 0], sq[:, :, 0:R], AX_X, ALU.add)
                    chain(dve.tensor_reduce(rinv[:, :, 1:3],
                                            sq[:, :, R:].rearrange("p t (g n) -> p t g n", n=NS), AX_X, ALU.add))
                    dve.tensor_scalar(rinv[:, :, 0], rinv[:, :, 0], 1.0 / R, RMS_EPS, ALU.mult, ALU.add)
                    chain(dve.tensor_scalar(rinv[:, :, 1:3], rinv[:, :, 1:3], 1.0 / NS, RMS_EPS, ALU.mult, ALU.add))
                    dve.sem_inc(ms_ready, 1)
                if stage == "rmsn":
                    dve.wait_ge(rinv_ready, c + 1)
                    for t in range(TT):
                        for g, (a, b) in enumerate(((0, R), (R, R + NS), (R + NS, XW))):
                            ins = dve.scalar_tensor_tensor(
                                out=ssn[c % 2][:, t, a:b], in0=ss[:, t, a:b], scalar=rinv[:, t, g:g + 1],
                                in1=rows[:, R_LN + a:R_LN + b], op0=ALU.mult, op1=ALU.mult)
                    ins.then_inc(ssn_ready, 1)
                if stage == "delta":
                    dve.wait_ge(log_ready, c + 1)
                    if c >= 1:
                        dve.wait_ge(decay_ready, NS * c)
                    for q in range(PAIRS):
                        ins = dve.scalar_tensor_tensor(
                            out=delta[:, 2 * q:2 * q + 2, :].rearrange("p d t -> p (d t)"),
                            in0=psum(f"dt{q}.{c}")[:, :], scalar=0.0,
                            in1=xh[:, 2 * q:2 * q + 2, :].rearrange("p d t -> p (d t)"),
                            op0=ALU.max, op1=ALU.add)
                        ins.then_inc(delta_ready, 1)
                    for q in range(PAIRS):
                        dve.wait_ge(delta_ready, PAIRS * c + q + 1)
                        dve.sem_inc(free(f"dt{q}.{c}"), 1)
                    if c >= 1:
                        dve.tensor_tensor(inj[c % 2][:], dcols[:, AC:AC + NS * KD].rearrange("p (n d) -> p n d", n=NS),
                                          delta[:, :, 0:1].rearrange("p d o -> p o d").broadcast_to([P, NS, KD]),
                                          ALU.mult).then_inc(first_ready, 1)

            def back(c, stage):
                uc = u[c % 2]
                if stage == "skip":
                    for q in range(PAIRS):
                        wait_job(dve, f"y{q}.{c}")
                        for i in range(2):
                            d = 2 * q + i
                            ins = dve.scalar_tensor_tensor(
                                out=uc[:, d, :], in0=uc[:, d, :], scalar=dcols[:, DP + d:DP + d + 1],
                                in1=psum(f"y{q}.{c}")[:, i * TC:(i + 1) * TC], op0=ALU.mult, op1=ALU.add)
                            if i == 0:
                                continue
                        chain(ins)
                        dve.sem_inc(free(f"y{q}.{c}"), 1)
                if stage[0] == "e":
                    q = int(stage[1])
                    dve.wait_ge(gth_ready, 4 * c + q + 1)
                    chain(dve.scalar_tensor_tensor(
                        out=xh[:, 2 * q:2 * q + 2, :].rearrange("p i t -> p (i t)"),
                        in0=gth[q % 2][:].rearrange("p i t -> p (i t)"), scalar=1.0, in1=psum(f"g{q}.{c}")[:, :],
                        op0=ALU.add, op1=ALU.mult))
                    dve.sem_inc(early_ready, 1)
                    dve.sem_inc(free(f"g{q}.{c}"), 1)
                if stage[0] == "z" and c == CHUNKS - 1:
                    q = int(stage[1])
                    pair = lambda a: a[:, 2 * q:2 * q + 2, :].rearrange("p i t -> p (i t)")
                    dve.scalar_tensor_tensor(out=pair(uc), in0=pair(xh), scalar=0.5, in1=pair(uc),
                                             op0=ALU.mult, op1=ALU.mult).then_inc(z_ready, 1)
                elif stage[0] == "z":
                    for q in (int(stage[1]),):
                        dve.wait_ge(gth_ready, 4 * c + q + 1)
                        g2 = gth[q % 2][:].rearrange("p i t -> p (i t)")
                        chain(dve.scalar_tensor_tensor(out=g2, in0=g2, scalar=1.0, in1=psum(f"g{q}.{c}")[:, :],
                                                       op0=ALU.add, op1=ALU.mult))
                        dve.sem_inc(free(f"g{q}.{c}"), 1)
                        z = uc[:, 2 * q:2 * q + 2, :].rearrange("p i t -> p (i t)")
                        dve.scalar_tensor_tensor(out=z, in0=g2, scalar=0.5, in1=z,
                                                 op0=ALU.mult, op1=ALU.mult).then_inc(z_ready, 1)
                if stage in ("o0", "o1"):
                    t = int(stage[1])
                    name = f"o{t}.{c}"
                    wait_job(dve, name)
                    if t == 0:
                        dve.wait_ge(xres_loaded, 16 * (c + 1))
                    chain(dve.tensor_tensor(xres[:, t, :], xres[:, t, :], psum(name)[:, :], ALU.add))
                    dve.sem_inc(free(name), 1)
                if stage == "stats":
                    norm_stats(xres)
                if stage == "norm":
                    for j in range(2):
                        wait_job(dve, f"lnT{j}.{c + 2}" if c + 2 < CHUNKS else f"l2T{j}.{c - 1}")
                    normalise(xres)
                if stage == "gate1":
                    name = f"gh.{c}"
                    wait_job(dve, name)
                    chain(dve.tensor_tensor(gh[:], rows[:, None, R_GB1:R_GB1 + GH].broadcast_to([P, TT, GH]),
                                            psum(name)[:, 0:TT * GH].rearrange("p (t n) -> p t n", t=TT), ALU.add))
                    dve.sem_inc(free(name), 1)
                    for t in range(TT):
                        ins = dve.bn_stats(stat2[:, t, :], gh[:, t, :])
                    chain(ins)
                    for t in range(TT):
                        ins = dve.bn_aggr(mv2[:, t, :], stat2[:, t, :])
                    chain(ins)
                    dve.tensor_scalar(rstd2[:], mv2[:, :, 1:2], LN_EPS, None, ALU.add).then_inc(gvar_ready, 1)
                if stage == "gate2":
                    dve.wait_ge(grstd_ready, c + 1)
                    for t in range(TT):
                        ins = dve.tensor_scalar(gh[:, t, :], gh[:, t, :], mv2[:, t, 0:1], rstd2[:, t, :],
                                                ALU.subtract, ALU.mult)
                    chain(ins)
                    chain(dve.tensor_tensor(gh[:], gh[:], rows[:, None, R_GAM:R_GAM + GH].broadcast_to([P, TT, GH]),
                                            ALU.mult))
                    chain(dve.tensor_tensor(gh[:], gh[:], rows[:, None, R_BET:R_BET + GH].broadcast_to([P, TT, GH]),
                                            ALU.add))
                    dve.tensor_scalar(gh[:], gh[:], 0.0, None, ALU.max).then_inc(gh_ready, 1)
                if stage in ("m0", "m1"):
                    t = int(stage[1])
                    name = f"m{t}.{c}"
                    wait_job(dve, name)
                    chain(dve.tensor_tensor(xres[:, t, :], xres[:, t, :], psum(name)[:, :], ALU.add))
                    dve.sem_inc(x2m_ready, 1)
                    dve.sem_inc(free(name), 1)
                if stage == "top":
                    name = f"gt.{c}"
                    wait_job(dve, name)
                    chain(dve.tensor_tensor(gates[:], rows[:, None, R_GB2:R_GB2 + NE].broadcast_to([P, TT, NE]),
                                            psum(name)[:, 0:TT * NE].rearrange("p (t n) -> p t n", t=TT), ALU.add))
                    dve.sem_inc(free(name), 1)
                    for t in range(TT):
                        ins = dve.max(topv[:, TT * c + t, :], gates[:, t, :])
                    chain(ins)
                    for t in range(TT):
                        ins = dve.max_index(topi[:, TT * c + t, :], topv[:, TT * c + t, :], gates[:, t, :])
                    chain(ins)

            def keep_last(g):
                if g < UNITS - NS:
                    dve.wait_ge(scanned, g + 1)
                    dve.tensor_copy(carry[:, g % NS, :].rearrange("p (d o) -> p d o", o=1),
                                    drive[g % N_DRIVE][:, :, TC - 1:TC]).then_inc(carried, 1)

            def scan(g):
                dve.wait_ge(decay_ready, g + 1)
                dve.wait_ge(drive_ready, g + 1)
                v = drive[g % N_DRIVE]
                if g >= NS:
                    chain(dve.tensor_tensor(v[:, :, 0:1], v[:, :, 0:1],
                                            inj[g // NS % 2][:, g % NS, :].rearrange("p (d o) -> p d o", o=1), ALU.add))
                flat = v.rearrange("p d t -> p (d t)")
                dve.tensor_tensor_scan(flat, decay[g % N_DECAY].rearrange("p d t -> p (d t)"), flat, 0.0,
                                       ALU.mult, ALU.add).then_inc(scanned, 1)

            def add_states(g):
                c, n = g // NS, g % NS
                for t in range(TT):
                    k = TT * g + t
                    dve.wait_ge(turned, k + 1)
                    cn = ssn[c % 2][:, t, R + NS + n:R + NS + n + 1]
                    if n == 0:
                        if t == 0 and c >= 1:
                            for q in range(PAIRS):
                                wait_job(dve, f"y{q}.{c - 1}")
                        dve.tensor_scalar(acc[:, t, :], stT[k % 2][:], cn, None, ALU.mult).then_inc(added, 1)
                    else:
                        dve.wait_ge(added, k - 1)
                        dve.scalar_tensor_tensor(out=acc[:, t, :], in0=stT[k % 2][:], scalar=cn, in1=acc[:, t, :],
                                                 op0=ALU.mult, op1=ALU.add).then_inc(added, 1)

            def gate_row(name, dst):
                wait_job(dve, name)
                ps = psum(name)
                chain(dve.tensor_scalar(dst[:], ps[:, :], 0.0, 2.0, ALU.is_ge, ALU.mult))
                chain(dve.tensor_scalar(dst[:], dst[:], -1.0, None, ALU.add))
                chain(dve.tensor_scalar(tmp, ps[:, :], -1.0, None, ALU.mult))
                chain(dve.scalar_tensor_tensor(out=tmp, in0=ps[:, :], scalar=0.25, in1=tmp,
                                               op0=ALU.max, op1=ALU.max))
                dve.sem_inc(free(name), 1)
                chain(dve.tensor_tensor(dst[:], dst[:], tmp, ALU.mult))
                dve.sem_inc(gates_ready, 1)

            def mod_cols(name, i, n_ready):
                wait_job(dve, name)
                chain(dve.tensor_copy(mcol[:, i, :], psum(name)[:, 0:KH]))
                chain(dve.tensor_scalar(mcol[:, i + 1, :], psum(name)[:, KH:2 * KH], 1.0, None, ALU.add))
                dve.sem_inc(free(name), 1)
                dve.sem_inc(mcol_ready, 1)

            wait_load(dve, "c")
            chain(dve.tensor_scalar(ccol[:, 2, :], ccol[:, 0, :], 0.5, None, ALU.mult))
            dve.wait_ge(c_tanh, 1)
            chain(dve.scalar_tensor_tensor(out=ccol[:, 2, :], in0=ccol[:, 1, :], scalar=1.0, in1=ccol[:, 2, :],
                                           op0=ALU.add, op1=ALU.mult))
            dve.tensor_copy(cbc, ccol[:, 2, :].rearrange("p (k o) -> p k o", o=1).broadcast_to([P, KH, P])
                            ).then_inc(c_ready, 1)
            wait_load(dve, "consts")
            dve.tensor_scalar(dcols[:, CW:DP], dcols[:, CW:DP], 0.5, None, ALU.mult).then_inc(c_ready, 1)
            dve.wait_ge(c_ready, 2)
            dve.wait_ge(consts_set, 1)
            for c, slot in slots():
                g = c * NS + slot
                if 0 < g <= UNITS:
                    if slot == 0 and g < UNITS:
                        keep_last(g - 1)
                        dve.wait_ge(carried, NS * c)
                        dve.wait_ge(first_exp, c)
                        chain(dve.tensor_tensor(inj[c % 2][:], inj[c % 2][:], carry[:], ALU.mult))
                if 0 <= g < UNITS:
                    scan(g)
                if c == -1 and slot == 3:
                    mod_cols("modA", 0, 1)
                stages(VECTOR_STAGES, c, slot, front, back)
                if c == -1 and slot == 11:
                    gate_row("modga", gar)
                    mod_cols("modB", 2, 2)
                    gate_row("modgb", gbr)
                if c == -1 and slot == 14:
                    for q in range(PAIRS):
                        s = slice(2 * q, 2 * q + 2)
                        dve.wait_ge(delta_ready, q + 1)
                        ins = dve.tensor_tensor(du[:, s, :], delta[:, s, :], u[0][:, s, :], ALU.mult)
                    ins.then_inc(du_ready, 1)
                if 0 < g <= UNITS:
                    if not (slot == 0 and g < UNITS):
                        keep_last(g - 1)
                    add_states(g - 1)
            chain(dve.tensor_copy(idx[:], topi[:, :, 0:TOPK]))
            dve.tensor_tensor(hot[:].rearrange("p t k e -> p (t k) e"),
                              idx[:].rearrange("p t (k o) -> p (t k) o", o=1).broadcast_to([P, NT * TOPK, NE]),
                              iota[:, None, :].broadcast_to([P, NT * TOPK, NE]), ALU.is_equal).then_inc(hot_ready, 1)
            dve.tensor_tensor(ediff[:, :, 0:1], topv[:, :, 1:2], topv[:, :, 0:1], ALU.subtract).then_inc(diff_ready, 1)
            dve.wait_ge(ediff_ready, 1)
            chain(dve.tensor_scalar(prob[:, :, 0:1], ediff[:, :, 1:2], 1.0, None, ALU.add))
            chain(dve.reciprocal(prob[:, :, 0:1], prob[:, :, 0:1]))
            chain(dve.tensor_tensor(prob[:, :, 1:2], prob[:, :, 0:1], ediff[:, :, 1:2], ALU.mult))
            dve.wait_ge(hot_ready, 1)
            chain(dve.tensor_tensor(hotw.rearrange("p t k e -> p (t k) e"),
                                    hot[:].rearrange("p t k e -> p (t k) e"),
                                    prob[:].rearrange("p t (k o) -> p (t k) o", o=1).broadcast_to([P, NT * TOPK, NE]),
                                    ALU.mult))
            wait_job(dve, "count")
            chain(dve.tensor_scalar(allowed[:].rearrange("p k e -> p (k e)"), psum("count")[:, 0:TOPK * NE],
                                    float(CAP), None, ALU.is_le))
            dve.sem_inc(free("count"), 1)
            chain(dve.tensor_tensor(hotw.rearrange("p t k e -> p t (k e)"),
                                    hotw.rearrange("p t k e -> p t (k e)"),
                                    allowed[:].rearrange("p k e -> p (k e)")[:, None, :].broadcast_to([P, NT, TOPK * NE]),
                                    ALU.mult))
            chain(dve.tensor_tensor(wexp, hotw[:, :, 0, :], hotw[:, :, 1, :], ALU.add))
            dve.wait_ge(lt_ready, CHUNKS)
            dve.scalar_tensor_tensor(
                out=lw.rearrange("p t (e r) -> p (t e) r", e=NE),
                in0=lt[:].rearrange("p t (e r) -> p (t e) r", e=NE), scalar=ALPHA,
                in1=wexp.rearrange("p t (e o) -> p (t e) o", o=1).broadcast_to([P, NT * NE, ER]),
                op0=ALU.mult, op1=ALU.mult).then_inc(lw_ready, 1)
            back(CHUNKS - 1, "m0")
            back(CHUNKS - 1, "m1")
            dve.wait_ge(x2_back, 16)
            for t in range(NT):
                name = f"lo{t}"
                wait_job(dve, name)
                if t >= 4:
                    dve.wait_ge(out_stored[t % 4], 16 * (t // 4))
                x2 = x2r[:, t, :] if t < NT - TT else xres[:, t - (NT - TT), :]
                chain(dve.tensor_tensor(fin[:, t % 4, :], x2, psum(name)[:, :], ALU.add))
                dve.sem_inc(fin_ready, 1)
                dve.sem_inc(free(name), 1)


def kernel(**inputs):
    import numpy as np
    import concourse.bacc as bacc
    from concourse.bass_utils import run_bass_kernel_spmd

    a = {k: np.asarray(v) for k, v in inputs.items()}

    def tiles(m):
        return np.ascontiguousarray(m.reshape(-1, P, m.shape[1]).transpose(1, 0, 2))

    def cols(v):
        return v.reshape(KD, P, -1).transpose(1, 0, 2).reshape(P, -1)

    w_in = a["L0_attn_W_in"].T
    a_cols = a["L0_attn_A"].reshape(KD, P, NS).transpose(1, 2, 0).reshape(P, -1)
    arrays = {
        "x": a["L0_attn_hidden_states"].reshape(T, H),
        "w_in_u": tiles(w_in[:, :D]),
        "w_in_g": tiles(w_in[:, D:]),
        "dcols": np.concatenate([cols(a["L0_attn_conv_w"]), cols(a["L0_attn_conv_b"]),
                                 cols(a["L0_attn_D_param"]), a_cols], axis=1),
        "w_x": tiles(a["L0_attn_Wx"].T),
        "w_dt": np.concatenate([a["L0_attn_Wdt"].T, a["L0_attn_dt_bias"][None, :]], axis=0),
        "w_out": tiles(a["L0_attn_W_out"].T),
        "w_ffn": tiles(a["L0_ffn_weight"].T),
        "lora_a": tiles(a["L0_ffn_lora_A"].transpose(1, 0, 2).reshape(H, NE * ER)),
        "lora_b": a["L0_ffn_lora_B"].reshape(NE * ER, H),
        "gw1": tiles(a["L0_ffn_gw1"].T),
        "gw2": a["L0_ffn_gw2"].T,
        "rows": np.concatenate([a["L0_attn_dt_ln_w"], a["L0_attn_b_ln_w"], a["L0_attn_c_ln_w"], a["L0_ffn_gb1"],
                                a["L0_ffn_ln_gamma"], a["L0_ffn_ln_beta"], a["L0_ffn_gb2"]])[None, :],
        "c": a["L0_c"].reshape(KH, P).T,
        "w_mod": tiles(a["L0_wmod"]),
        "ident": np.eye(P, dtype=np.float32),
        "iota": np.tile(np.arange(NE, dtype=np.float32), (P, 1)),
    }
    nc = bacc.Bacc("TRN2", target_bir_lowering=False, num_devices=1)
    named, args = {}, []
    for name, v in arrays.items():
        v = np.ascontiguousarray(v)
        named[f"in_{name}"] = v
        args.append(nc.dram_tensor(f"in_{name}", v.shape, mybir.dt.from_np(v.dtype), kind="ExternalInput").ap())
    args.append(nc.dram_tensor("out", (T, H), F32, kind="ExternalOutput").ap())
    adaln_block(nc, *args)
    r = run_bass_kernel_spmd(nc, [named], core_ids=[0])
    return r.results[0]["out"].reshape(1, T, H)
```

```python
from contextlib import ExitStack

import concourse.bass as bass
from concourse import mybir

F32 = mybir.dt.float32
U32 = mybir.dt.uint32
ALU = mybir.AluOpType
ACT = mybir.ActivationFunctionType
AX_X = mybir.AxisListType.X

P = 128
T = 1024
H = 512
D = 1024
NS = 16
R = 32
KW = 4
NE, TOPK, ER, GH = 8, 2, 16, 32
CAP = int(3.0 * T / NE)
ALPHA = 1.0 / ER
RMS_EPS, LN_EPS = 1e-6, 1e-5

TC = 256
CHUNKS = T // TC
TT = TC // P
NT = T // P
KH = H // P
KD = D // P
PAIRS = KD // 2
UNITS = CHUNKS * NS
SLOTS = NS
LOAD_SLOT = 12
SIDE = 4
N_DRIVE, N_DECAY, N_BREP = 3, 3, 2
NB = 2
XW = R + 2 * NS
CW, CB, DP, AC = 0, KD * KW, KD * KW + KD, KD * KW + 2 * KD
DCOLS = AC + NS * KD
R_LN, R_GB1, R_GAM, R_BET, R_GB2 = 0, XW, XW + GH, XW + 2 * GH, XW + 3 * GH
ROWS = R_GB2 + NE
SA, CA, GA, SB, CBM, GB = range(6)


LAST = CHUNKS - 1
TENSOR_STAGES = {
    1: ["b:y", "b:g2"], 3: ["b:g3", "f:lnT"], 4: ["f:u0"], 5: ["f:u1", "f:u2"], 6: ["b:oa0", "f:u3", "b:ob0"],
    7: ["b:oa1", "b:ob1"], 8: ["n:g0"], 9: ["f:xp"], 10: ["f:xpT", "b:l2T0", "b:l2T1"],
    11: ["b:gh0", "b:gh1", "b:ma0", "b:mb0"], 12: ["f:dbT", "b:ma1", "b:mb1", "f:dt"], 14: ["b:la0", "b:la1", "n:g1"],
    15: ["b:ghT", "b:gt"],
    (0, 3): ["f:lnT"], (0, 4): ["f:u0"], (0, 5): ["f:u1", "f:u2"], (0, 6): ["f:u3"], (0, 8): ["n:g0"],
    (0, 9): ["f:xp"], (0, 10): ["f:xpT"], (0, 12): ["f:dbT", "f:dt"], (0, 14): ["n:g1"],
    (LAST, 1): ["b:y"], (LAST, 2): ["b:g2"], (LAST, 3): ["b:g3"], (LAST, 4): ["f:u0", "b:oa0"], (LAST, 6): ["b:ob0"],
    (LAST, 7): ["b:oa1", "b:ob1"], (LAST, 9): ["f:u1"], (LAST, 10): ["b:l2T0", "b:l2T1"],
    (LAST, 11): ["b:gh0", "b:gh1", "b:ma0", "b:mb0"], (LAST, 12): ["b:la0", "b:ma1", "b:mb1"],
    (LAST, 13): ["b:la1", "f:u2"], (LAST, 14): ["f:u3"], (LAST, 15): ["b:ghT", "b:gt"],
    (CHUNKS, 1): ["b:y"], (CHUNKS, 5): ["b:oa0"], (CHUNKS, 7): ["b:ob0", "b:oa1", "b:ob1"],
    (CHUNKS, 10): ["b:l2T0", "b:gh0", "b:la0", "b:l2T1", "b:gh1", "b:la1", "b:ma0"], (CHUNKS, 12): ["b:ghT"],
    (CHUNKS, 14): ["b:gt"], (CHUNKS, 15): ["b:mb0", "b:count", "b:ma1", "b:mb1"]}
SCALAR_STAGES = {
    1: ["f:norm"], 3: ["b:g2", "f:lnT"], 4: ["b:g3", "f:u0", "f:u1"], 5: ["f:u2"], 6: ["f:u3"], 7: ["b:o0"],
    8: ["b:o1", "f:tanh0", "f:tanh1", "n:g0"], 9: ["f:xp", "b:norm0", "b:norm1", "b:l2T0"], 10: ["b:l2T1"],
    11: ["f:dbT", "b:m0"], 13: ["b:m1", "f:log"], 14: ["b:ghT", "n:g1"], 15: ["b:la", "f:first"],
    (0, 1): ["f:norm"], (0, 3): ["f:lnT"], (0, 4): ["f:u0", "f:u1"], (0, 5): ["f:u2"], (0, 6): ["f:u3"],
    (0, 8): ["f:tanh0", "f:tanh1", "n:g0"], (0, 9): ["f:xp"], (0, 13): ["f:dbT", "f:log"], (0, 14): ["n:g1"],
    (0, 15): ["f:first"],
    (LAST, 3): ["b:g2"], (LAST, 4): ["b:g3", "f:u0"], (LAST, 5): ["b:o0"], (LAST, 8): ["b:o1"],
    (LAST, 9): ["b:norm0", "b:norm1", "f:u1"], (LAST, 10): ["b:l2T0", "b:l2T1"], (LAST, 11): ["b:m0"],
    (LAST, 13): ["b:m1", "b:la", "f:u2"], (LAST, 14): ["b:ghT", "f:u3"],
    (CHUNKS, 8): ["b:norm0", "b:l2T0", "b:norm1", "b:l2T1"], (CHUNKS, 13): ["b:la"], (CHUNKS, 14): ["b:ghT"]}
VECTOR_STAGES = {
    0: ["f:stats"], 1: ["b:skip0", "b:skip1"], 2: ["b:skip2", "b:skip3"], 3: ["b:z2"], 4: ["b:z3"], 5: ["f:conv0"],
    6: ["f:conv1", "f:conv2"], 7: ["f:conv3", "b:st0"], 8: ["b:st1", "f:silu0", "f:silu1"], 9: ["n:z0"],
    10: ["f:rms"], 11: ["f:rmsn", "b:gate1"], 13: ["f:delta"], 14: ["b:gate2"], 15: ["b:top", "n:z1"],
    (0, 0): ["f:stats"], (0, 5): ["f:conv0"], (0, 6): ["f:conv1", "f:conv2"], (0, 7): ["f:conv3"],
    (0, 8): ["f:silu0", "f:silu1"], (0, 9): ["n:z0"], (0, 10): ["f:rms"], (0, 11): ["f:rmsn"], (0, 13): ["f:delta"],
    (0, 15): ["n:z1"],
    (LAST, 1): ["b:skip0", "b:skip1"], (LAST, 2): ["b:skip2", "b:skip3"], (LAST, 3): ["b:z2"], (LAST, 4): ["b:z3"],
    (LAST, 7): ["b:st0", "f:conv0"], (LAST, 8): ["b:st1"], (LAST, 10): ["f:conv1"], (LAST, 11): ["b:gate1"],
    (LAST, 12): ["b:gate2"], (LAST, 14): ["f:conv2"], (LAST, 15): ["b:top", "f:conv3"],
    (CHUNKS, 1): ["b:skip0", "b:z0", "b:skip1", "b:z1", "b:skip2", "b:z2", "b:skip3", "b:z3"],
    (CHUNKS, 8): ["b:o0", "b:st0", "b:o1", "b:st1"], (CHUNKS, 10): ["b:gate1"], (CHUNKS, 11): ["b:gate2", "b:top"]}
POOL_STAGES = {
    0: ["f:rstd", "b:z0"], 3: ["b:z1", "b:z2"], 4: ["b:z3"], 8: ["b:rstd0", "b:rstd1"], 10: ["f:rms"],
    12: ["b:rgate"],
    (0, 1): ["f:rstd"], (0, 10): ["f:rms"],
    (LAST, 1): ["b:z0", "b:z1"], (LAST, 4): ["b:z2", "b:z3"], (LAST, 8): ["b:rstd0", "b:rstd1"],
    (LAST, 10): ["b:rgate"],
    (CHUNKS, 3): ["b:rstd0"], (CHUNKS, 6): ["b:rstd1"], (CHUNKS, 15): ["b:rgate"]}
SCALAR_STAGES_FIRST = (2, 8, 10, 13, 15)
VECTOR_STAGES_FIRST = (6, 7, 8, 12)
JOBS_OF = {"y": ["y0", "y1", "y2", "y3"], "lnT": ["lnT0", "lnT1"], "gh0": ["gh"], "gh1": [], "la0": ["la"], "la1": [],
           "oa0": ["o0"], "ob0": [], "oa1": ["o1"], "ob1": [], "ma0": ["m0"], "mb0": [], "ma1": ["m1"], "mb1": [],
           "dt": ["dt0", "dt1", "dt2", "dt3"]}


EARLY = {"u0": "g0", "u1": "g1", "u2": "g2", "u3": "g3", "conv0": "e0", "conv1": "e1", "conv2": "e2", "conv3": "e3"}


def chunk_stages(table, c, slot):
    for stage in table.get((c, slot) if c == 0 or c >= CHUNKS - 1 else slot, []):
        part, stage = stage.split(":")
        if part == "f" and c + 1 < CHUNKS:
            yield c + 1, stage
        if part == "f" and c + 1 == CHUNKS and stage in EARLY:
            yield c, EARLY[stage]
        if part == "n" and 0 <= c < CHUNKS - 1:
            yield c, stage
        if part == "b" and c >= 1 and not (c == CHUNKS and stage in ("g0", "g1", "g2", "g3")):
            yield c - 1, stage


def plan_jobs():
    names = []
    for c in range(-1, CHUNKS + 1):
        for slot in range(SLOTS):
            for of, stage in chunk_stages(TENSOR_STAGES, c, slot):
                names += [f"{j}.{of}" for j in JOBS_OF.get(stage, [stage])]
    names += [f"lwT{j}" for j in range(2)] + [f"lo{t}" for t in range(NT)]
    return {n: (i % SIDE, i // SIDE + 1) for i, n in enumerate(names)}


def adaln_block(nc, x, w_in_u, w_in_g, dcols_d, w_x, w_dt, w_out, w_ffn, lora_a, lora_b, gw1, gw2,
                rows_d, c_d, w_mod, ident_d, iota_d, out):
    jobs = plan_jobs()
    b_scratch = nc.dram_tensor("b_scratch", (CHUNKS, NS, TC), F32, kind="Internal").ap()
    x2_scratch = nc.dram_tensor("x2_scratch", (T, H), F32, kind="Internal").ap()

    with ExitStack() as ctx:
        def sb(name, shape, dt=F32):
            return ctx.enter_context(nc.sbuf_tensor(name, shape, dt))

        def sem(name):
            return ctx.enter_context(nc.semaphore(name))

        wu = sb("wu", [P, KH, D])
        wg = sb("wg", [P, KH, D])
        wo = sb("wo", [P, KD, H])
        wf = sb("wf", [P, KH, H])
        wla = sb("wla", [P, KH, NE * ER])
        wlb = sb("wlb", [P, H])
        wx = sb("wx", [P, KD, XW])
        wdt = sb("wdt", [R + 1, D])
        wg1 = sb("wg1", [P, KH, GH])
        wg2 = sb("wg2", [GH, NE])
        dcols = sb("dcols", [P, DCOLS])
        rows = sb("rows", [P, ROWS])
        ident = sb("ident", [P, P])
        iota = sb("iota", [P, NE])
        ones = sb("ones", [P, P])
        ccol = sb("ccol", [P, 3, KH])
        mcol = sb("mcol", [P, 4, KH])
        big = sb("big", [P, N_DRIVE + N_DECAY + 1, KD * TC])
        wmod = big[:, 0:6, :].rearrange("p a b -> p (a b)").rearrange("p (k n) -> p k n", k=KH)
        drive = [big[:, i, :].rearrange("p (d t) -> p d t", d=KD) for i in range(N_DRIVE)]
        acc = big[:, N_DRIVE, :].rearrange("p (t d) -> p t d", t=TT)
        decay = [big[:, N_DRIVE + 1 + i, :].rearrange("p (d t) -> p d t", d=KD) for i in range(N_DECAY)]
        x2r = big[:, 0:2, :].rearrange("p a b -> p (a b)").rearrange("p (t h) -> p t h", t=NT)[:, 0:NT - TT, :]
        lwT = big[:, N_DRIVE + 1, 0:NT * P].rearrange("p (t n) -> p t n", t=NT)
        lw = big[:, N_DRIVE + 2, 0:NT * P].rearrange("p (t n) -> p t n", t=NT)
        fin = big[:, N_DRIVE, :].rearrange("p (b h) -> p b h", h=H)
        xn = sb("xn", [P, TT, H])
        hT = [sb(f"hT{i}", [P, KH, TC]) for i in range(2)]
        upre = [sb(f"upre{i}", [P, 2, KW - 1 + TC]) for i in range(2)]
        halo = sb("halo", [P, KD, KW - 1])
        step = [sb(f"step{i}", [P, KD, TC]) for i in range(2)]
        u = [sb(f"u{i}", [P, KD, TC]) for i in range(2)]
        ssT = upre[0][0:XW, 0, 0:TC]
        bT = upre[1][0:R + NS, 0, 0:TC]
        ghT = upre[1][0:GH, 1, 0:TC]
        ss = sb("ss", [P, TT, XW])
        sq = sb("sq", [P, TT, XW])
        ssn = [sb(f"ssn{i}", [P, TT, XW]) for i in range(2)]
        rinv = sb("rinv", [P, TT, 3])
        dtT = sb("dtT", [R + 1, TC])
        du = sb("du", [P, KD, TC])
        brep = [sb(f"brep{i}", [P, NB, TC]) for i in range(N_BREP)]
        carry = sb("carry", [P, NS, KD])
        first = sb("first", [P, NS, KD])
        stat = sb("stat", [P, TT, 6])
        mv = sb("mv", [P, TT, 2])
        rstd = sb("rstd", [P, TT, 1])
        mhalf = sb("mhalf", [P, 8])
        xres = sb("xres", [P, TT, H])
        gth = [sb(f"gth{i}", [P, 2, TC]) for i in range(2)]
        h2T = sb("h2T", [P, KH, TC])
        tmp = gth[0][:].rearrange("p i t -> p (i t)")
        stat2 = sb("stat2", [P, TT, 6])
        mv2 = sb("mv2", [P, TT, 2])
        rstd2 = sb("rstd2", [P, TT, 1])
        gh = sb("gh", [P, TT, GH])
        gates = sb("gates", [P, TT, NE])
        lt = sb("lt", [P, NT, NE * ER])
        gar, gbr = [lt[:, 4 * i:4 * i + 4, :].rearrange("p t n -> p (t n)") for i in range(2)]
        topv = sb("topv", [P, NT, 8])
        topi = sb("topi", [P, NT, 8], U32)
        idx = sb("idx", [P, NT, TOPK])
        hot = sb("hot", [P, NT, TOPK, NE])
        hotw = big[:, N_DRIVE, 0:NT * TOPK * NE].rearrange("p (t k e) -> p t k e", k=TOPK, e=NE)
        allowed = sb("allowed", [P, TOPK, NE])
        prob = sb("prob", [P, NT, TOPK])
        ediff = sb("ediff", [P, NT, 2])
        wexp = big[:, 2, 0:NT * NE].rearrange("p (t e) -> p t e", e=NE)

        side = [ctx.enter_context(nc.psum_tensor(f"side{i}", [P, 512], F32)) for i in range(SIDE)]
        stT = [ctx.enter_context(nc.psum_tensor(f"stT{i}", [P, KD * P], F32)) for i in range(2)]

        bank_ready = [sem(f"bank_ready{i}") for i in range(SIDE)]
        bank_free = [sem(f"bank_free{i}") for i in range(SIDE)]
        loads = ["c", "ident", "consts", "wm0a", "wm0b", "wm1", "wm2", "wu0", "wu1", "wx", "wg", "wo", "wf",
                 "small", "lora"]
        loaded = {n: sem(f"ld_{n}") for n in loads}
        n_load = {}
        xin_loaded, xres_loaded = sem("xin_loaded"), sem("xres_loaded")
        x2_stored, x2_back = sem("x2_stored"), sem("x2_back")
        out_stored = [sem(f"out_stored{i}") for i in range(4)]
        b_stored = sem("b_stored")
        brep_loaded = [sem(f"brep_loaded{i}") for i in range(N_BREP)]
        dve_chain, pool_chain, act_chain = sem("dve_chain"), sem("pool_chain"), sem("act_chain")
        consts_set, c_tanh, taps_halved = sem("consts_set"), sem("c_tanh"), sem("taps_halved")
        mod_summed, mod_ready = sem("mod_summed"), sem("mod_ready")
        mcol_ready, gates_ready, scaled = sem("mcol_ready"), sem("gates_ready"), sem("scaled")
        var_ready, rstd_ready, xn_ready = sem("var_ready"), sem("rstd_ready"), sem("xn_ready")
        hT_ready, taps_ready = sem("hT_ready"), sem("taps_ready")
        conv_done, halo_saved = sem("conv_done"), sem("halo_saved")
        tanh_ready, u_ready = sem("tanh_ready"), sem("u_ready")
        ssT_ready, ms_ready = sem("ssT_ready"), sem("ms_ready")
        rinv_ready, ssn_ready = sem("rinv_ready"), sem("ssn_ready")
        bT_ready, dtT_ready = sem("bT_ready"), sem("dtT_ready")
        log_ready, du_ready = sem("log_ready"), sem("du_ready")
        first_ready, first_exp = sem("first_ready"), sem("first_exp")
        first_drive = sem("first_drive")
        decay_ready, drive_ready, scanned = sem("decay_ready"), sem("drive_ready"), sem("scanned")
        turned, added = sem("turned"), sem("added")
        gth_ready, z_ready = sem("gth_ready"), sem("z_ready")
        h2T_ready = sem("h2T_ready")
        gvar_ready, grstd_ready, gh_ready = sem("gvar_ready"), sem("grstd_ready"), sem("gh_ready")
        ghT_ready = sem("ghT_ready")
        lt_ready, hot_ready = sem("lt_ready"), sem("hot_ready")
        diff_ready, ediff_ready = sem("diff_ready"), sem("ediff_ready")
        lw_ready, lwT_ready = sem("lw_ready"), sem("lwT_ready")

        def psum(name):
            return side[jobs[name][0]]

        def wait_job(eng, name):
            bank, nth = jobs[name]
            eng.wait_ge(bank_ready[bank], nth)

        def free(name):
            return bank_free[jobs[name][0]]

        def release(ins, name):
            ins.then_inc(free(name), 1)

        def wait_released(eng, name):
            bank, nth = jobs[name]
            eng.wait_ge(bank_free[bank], nth)

        class Chain:

            def __init__(self, eng, s):
                self.eng, self.s, self.n = eng, s, 0

            def __call__(self, ins):
                self.n += 1
                ins.then_inc(self.s, 1)
                self.eng.wait_ge(self.s, self.n)

        def wait_load(eng, name):
            eng.wait_ge(loaded[name], 16 * n_load[name])

        def xn_front(c):
            return TT * (c + 1 + max(0, c - 2))

        def xn_back(c):
            return TT * (min(c + 3, CHUNKS) + c + 1)

        def slots():
            for c in range(-1, CHUNKS + 1):
                for slot in range(SLOTS):
                    yield c, slot

        def stages(table, c, slot, front, back):
            for of, stage in chunk_stages(table, c, slot):
                (front if of == c + 1 else back)(of, stage)

        def wait_mod_done(eng):
            eng.wait_ge(mod_ready, 4)

        block = ctx.enter_context(nc.Block())

        @block.sync
        def _(sp):
            def load(group, dst, src):
                n_load[group] = n_load.get(group, 0) + 1
                sp.dma_start(dst, src).then_inc(loaded[group], 16)

            load("c", ccol[:, 0, :], c_d)
            xt = x.rearrange("(c t p) h -> c p t h", p=P, t=TT)
            sp.dma_start(xn[:], xt[0]).then_inc(xin_loaded, 16)
            load("ident", ident[:], ident_d)
            load("wm0a", wmod[:, 0:2, 0:1024], w_mod[:, 0:2, 0:1024])
            load("wm0b", wmod[:, 2:4, 0:1024], w_mod[:, 2:4, 0:1024])
            load("wu0", wu[:, :, 0:D // 2], w_in_u[:, :, 0:D // 2])
            load("consts", iota[:], iota_d)
            load("consts", dcols[:], dcols_d)
            load("consts", rows[:], rows_d.broadcast_to([P, ROWS]))
            load("wu1", wu[:, :, D // 2:], w_in_u[:, :, D // 2:])
            load("wx", wx[:], w_x)
            load("wx", wdt[:], w_dt)
            load("wm1", wmod[:, :, 1024:2048], w_mod[:, :, 1024:2048])
            load("wm2", wmod[:, :, 2048:3072], w_mod[:, :, 2048:3072])
            load("wo", wo[:], w_out)
            load("wf", wf[:], w_ffn)
            load("lora", wla[:], lora_a)
            load("lora", wlb[:], lora_b)
            load("small", wg1[:], gw1)
            load("small", wg2[:], gw2)
            load("wg", wg[:], w_in_g)

            for c, slot in slots():
                if 0 <= c + 1 < CHUNKS - 1 and slot == (LOAD_SLOT if c >= 0 else 4):
                    for job in [f"lnT0.{c + 1}", f"lnT1.{c + 1}"] + ([f"l2T1.{c - 1}"] if c >= 1 else []):
                        wait_job(sp, job)
                    sp.dma_start(xn[:], xt[c + 2]).then_inc(xin_loaded, 16)
                if c >= 1 and slot == 0:
                    if c >= 2:
                        sp.wait_ge(x2_stored, 16 * (c - 1))
                    sp.dma_start(xres[:], xt[c - 1]).then_inc(xres_loaded, 16)
                if c + 1 < CHUNKS and slot == 13:
                    sp.wait_ge(bT_ready, c + 2)
                    sp.dma_start(b_scratch[c + 1], bT[R:R + NS, :]).then_inc(b_stored, 16)
                g = c * NS + slot + 2
                if g % NB == 0 and 0 <= g < UNITS:
                    j = g // NB
                    if g % NS == 0:
                        sp.wait_ge(b_stored, 16 * (g // NS + 1))
                    if j >= N_BREP:
                        sp.wait_ge(drive_ready, NB * (j - N_BREP) + NB - 1)
                        if j == N_BREP:
                            sp.wait_ge(first_drive, 1)
                    cc, n = g // NS, g % NS
                    src = b_scratch[cc:cc + 1, n:n + NB, :].broadcast_to([P, NB, TC])
                    sp.dma_start(brep[j % N_BREP][:], src).then_inc(brep_loaded[j % N_BREP], 16)
                if 1 <= c < CHUNKS and slot == 14:
                    for t in range(TT):
                        wait_released(sp, f"m{t}.{c - 1}")
                    sp.dma_start(x2_scratch.rearrange("(c t p) h -> c p t h", p=P, t=TT)[c - 1],
                                 xres[:]).then_inc(x2_stored, 16)
            sp.wait_ge(x2_stored, 16 * (CHUNKS - 1))
            sp.wait_ge(turned, TT * UNITS)
            sp.dma_start(x2r, x2_scratch[0:(NT - TT) * P, :].rearrange("(t p) h -> p t h", p=P)
                         ).then_inc(x2_back, 16)
            for t in range(NT):
                wait_released(sp, f"lo{t}")
                sp.dma_start(out[t * P:(t + 1) * P, :], fin[:, t % 4, :]).then_inc(out_stored[t % 4], 16)
            for i in range(4):
                sp.wait_ge(out_stored[i], 16 * NT // 4)

        @block.tensor
        def _(pe):
            def begin(name):
                bank, nth = jobs[name]
                if nth > 1:
                    pe.wait_ge(bank_free[bank], nth - 1)
                return side[bank]

            def end(name, ins):
                ins.then_inc(bank_ready[jobs[name][0]], 1)

            def mod_row(r):
                pe.wait_ge(mod_summed, r // 2 + 1)
                half = stT[0][:, 0:H] if r == GA else stT[1][:, H:2 * H]
                pe.matmul(half, ones[:], wmod[:, 0, r * H:(r + 1) * H], start=True, stop=True).then_inc(mod_ready, 1)

            def mod_cols(rows_, at):
                for i, r in enumerate(rows_):
                    pe.wait_ge(mod_summed, r // 2 + 1)
                    for m in range(KH):
                        f = r * H + m * P
                        last = pe.matmul(stT[1][:, at + i * KH + m:at + i * KH + m + 1], wmod[:, 0, f:f + P],
                                         ones[:, 0:1], start=True, stop=True)
                last.then_inc(mod_ready, 1)

            def turn_tokens(job, src, count):
                banks = [begin(job(j)) for j in range(2)]
                for t in range(TT):
                    pe.wait_ge(xn_ready, count - TT + t + 1)
                    for k in range(KH):
                        at = k % 2 * TC + t * P
                        last = pe.transpose(banks[k // 2][:, at:at + P], src[:, t, k * P:(k + 1) * P], ident[:])
                        if t == TT - 1 and k % 2 == 1:
                            end(job(k // 2), last)

            def project_pair(name, weights, q, rhs):
                ps = begin(name)
                for i in range(2):
                    d0 = (2 * q + i) * P
                    for k in range(KH):
                        last = pe.matmul(ps[:, i * TC:(i + 1) * TC], weights[:, k, d0:d0 + P], rhs[:, k, :],
                                         start=(k == 0), stop=(k == KH - 1))
                end(name, last)

            def front(c, stage):
                if stage == "lnT":
                    turn_tokens(lambda j: f"lnT{j}.{c}", xn, xn_front(c))
                    if c == 0:
                        mod_cols((SA, CA), 0)
                if stage[0] == "u":
                    pe.wait_ge(hT_ready, KH * (c + 1))
                    if c == 0:
                        wait_load(pe, "wu0" if stage in ("u0", "u1") else "wu1")
                    project_pair(f"{stage}.{c}", wu, int(stage[1]), hT[c % 2])
                if stage == "xp":
                    ps = begin(f"xp.{c}")
                    if c == 0:
                        wait_load(pe, "wx")
                    for k in range(KD):
                        if k % (KD // 2) == 0:
                            pe.wait_ge(u_ready, 2 * c + k // (KD // 2) + 1)
                        last = pe.matmul(ps[0:XW, 0:TC], wx[:, k, :], u[c % 2][:, k, :],
                                         start=(k == 0), stop=(k == KD - 1))
                    end(f"xp.{c}", last)
                if stage == "xpT":
                    ps = begin(f"xpT.{c}")
                    pe.wait_ge(ssT_ready, c + 1)
                    for t in range(TT):
                        last = pe.transpose(ps[:, t * XW:(t + 1) * XW], ssT[:, t * P:(t + 1) * P],
                                            ident[0:XW, 0:XW])
                    end(f"xpT.{c}", last)
                if stage == "dbT":
                    if c == 0:
                        mod_row(GA)
                    ps = begin(f"dbT.{c}")
                    pe.wait_ge(ssn_ready, c + 1)
                    for t in range(TT):
                        last = pe.transpose(ps[0:R + NS, t * P:(t + 1) * P], ssn[c % 2][:, t, 0:R + NS], ident[:])
                    end(f"dbT.{c}", last)
                if stage == "dt":
                    pe.wait_ge(dtT_ready, c + 1)
                    for q in range(PAIRS):
                        ps = begin(f"dt{q}.{c}")
                        for i in range(2):
                            d0 = (2 * q + i) * P
                            last = pe.matmul(ps[:, i * TC:(i + 1) * TC], wdt[:, d0:d0 + P], dtT[:, :],
                                             start=True, stop=True)
                        end(f"dt{q}.{c}", last)
                    if c == 0:
                        mod_cols((SB, CBM), 2 * KH)
                        mod_row(GB)

            def residual(ps, c, t):
                if c < CHUNKS - 1:
                    pe.matmul(ps[:, :], ident[:], xres[:, t, :], start=True, stop=False)

            def back(c, stage):
                if stage == "y":
                    banks = [begin(f"y{q}.{c}") for q in range(PAIRS)]
                    for t in range(TT):
                        pe.wait_ge(added, TT * NS * (c + 1) - TT + t + 1)
                        for q in range(PAIRS):
                            for i in range(2):
                                d0 = (2 * q + i) * P
                                last = pe.transpose(banks[q][:, i * TC + t * P:i * TC + (t + 1) * P],
                                                    acc[:, t, d0:d0 + P], ident[:])
                            if t == TT - 1:
                                end(f"y{q}.{c}", last)
                if stage in ("g0", "g1", "g2", "g3"):
                    wait_load(pe, "wg")
                    project_pair(f"{stage}.{c}", wg, int(stage[1]), hT[c % 2])
                if stage[0] == "o":
                    t, first = int(stage[2]), stage[1] == "a"
                    ps = begin(f"o{t}.{c}") if first else psum(f"o{t}.{c}")
                    pe.wait_ge(scaled, KD)
                    if first:
                        pe.wait_ge(xres_loaded, 16 * (c + 1))
                        residual(ps, c, t)
                    for k in range(KD)[:KD // 2] if first else range(KD)[KD // 2:]:
                        if t == 0 and k % 2 == 0:
                            pe.wait_ge(z_ready, PAIRS * c + k // 2 + 1)
                        last = pe.matmul(ps[:, :], u[c % 2][:, k, t * P:(t + 1) * P], wo[:, k, :],
                                         start=(k == 0 and c == CHUNKS - 1), stop=(k == KD - 1))
                    if not first:
                        end(f"o{t}.{c}", last)
                if stage in ("l2T0", "l2T1"):
                    t = int(stage[3])
                    ps = begin(f"{stage}.{c}")
                    pe.wait_ge(xn_ready, xn_back(c) - TT + t + 1)
                    for k in range(KH):
                        last = pe.transpose(ps[:, k * P:(k + 1) * P], xn[:, t, k * P:(k + 1) * P], ident[:])
                    end(f"{stage}.{c}", last)
                if stage in ("gh0", "gh1"):
                    t = int(stage[2])
                    ps = begin(f"gh.{c}") if t == 0 else psum(f"gh.{c}")
                    pe.wait_ge(h2T_ready, KH * (TT * c + t + 1))
                    wait_load(pe, "small")
                    wait_load(pe, "lora")
                    for k in range(KH):
                        last = pe.matmul(ps[:, t * GH:(t + 1) * GH], h2T[:, k, t * P:(t + 1) * P],
                                         wg1[:, k, :], start=(k == 0), stop=(k == KH - 1))
                    if t == TT - 1:
                        end(f"gh.{c}", last)
                if stage in ("la0", "la1"):
                    t = int(stage[2])
                    ps = begin(f"la.{c}") if t == 0 else psum(f"la.{c}")
                    for k in range(KH):
                        last = pe.matmul(ps[:, t * P:(t + 1) * P], h2T[:, k, t * P:(t + 1) * P],
                                         wla[:, k, :], start=(k == 0), stop=(k == KH - 1))
                    if t == TT - 1:
                        end(f"la.{c}", last)
                if stage[:2] in ("ma", "mb"):
                    t, first = int(stage[2]), stage[1] == "a"
                    ps = begin(f"m{t}.{c}") if first else psum(f"m{t}.{c}")
                    pe.wait_ge(scaled, KD + KH + 1)
                    if first:
                        residual(ps, c, t)
                    for k in range(KH)[:KH // 2] if first else range(KH)[KH // 2:]:
                        last = pe.matmul(ps[:, :], h2T[:, k, t * P:(t + 1) * P], wf[:, k, :],
                                         start=(k == 0 and c == CHUNKS - 1), stop=(k == KH - 1))
                    if not first:
                        end(f"m{t}.{c}", last)
                if stage == "count":
                    ps = begin(f"count.{c}")
                    pe.wait_ge(hot_ready, 1)
                    for t in range(NT):
                        last = pe.matmul(ps[:, 0:TOPK * NE], ones[:], hot[:, t, :, :].rearrange("p k e -> p (k e)"),
                                         start=(t == 0), stop=(t == NT - 1))
                    end(f"count.{c}", last)
                if stage == "ghT":
                    ps = begin(f"ghT.{c}")
                    pe.wait_ge(gh_ready, c + 1)
                    for t in range(TT):
                        last = pe.transpose(ps[0:GH, t * P:(t + 1) * P], gh[:, t, :], ident[:])
                    end(f"ghT.{c}", last)
                if stage == "gt":
                    ps = begin(f"gt.{c}")
                    pe.wait_ge(ghT_ready, c + 1)
                    for t in range(TT):
                        last = pe.matmul(ps[:, t * NE:(t + 1) * NE], ghT[:, t * P:(t + 1) * P], wg2[:, :],
                                         start=True, stop=True)
                    end(f"gt.{c}", last)

            pe.wait_ge(consts_set, 1)
            wait_load(pe, "ident")
            for c, slot in slots():
                stages(TENSOR_STAGES, c, slot, front, back)
                if 0 <= c < CHUNKS:
                    g = c * NS + slot
                    for t in range(TT):
                        k = TT * g + t
                        pe.wait_ge(scanned, g + 1)
                        if k >= 2:
                            pe.wait_ge(added, k - 1)
                        else:
                            pe.wait_ge(gates_ready, k + 1)
                        for d in range(KD):
                            last = pe.transpose(stT[k % 2][:, d * P:(d + 1) * P],
                                                drive[g % N_DRIVE][:, d, t * P:(t + 1) * P], ident[:])
                        last.then_inc(turned, 1)
            pe.wait_ge(lw_ready, 1)
            for j in range(2):
                ps = begin(f"lwT{j}")
                for i in range(NT // 2):
                    last = pe.transpose(ps[:, i * P:(i + 1) * P], lw[:, j * NT // 2 + i, :], ident[:])
                end(f"lwT{j}", last)
            for t in range(NT):
                ps = begin(f"lo{t}")
                pe.wait_ge(lwT_ready, t // (NT // 2) + 1)
                end(f"lo{t}", pe.matmul(ps[:, :], lwT[:, t, :], wlb[:, :], start=True, stop=True))

        @block.scalar
        def _(act):
            def evacuate_norm(job, dst, shift, ready, n):
                for j in range(2):
                    wait_job(act, job(j))
                    for i in range(2):
                        k = 2 * j + i
                        ins = act.activation(dst[:, k, :], psum(job(j))[:, i * TC:(i + 1) * TC], ACT.Identity,
                                             bias=mcol[:, shift, k:k + 1], scale=mcol[:, shift + 1, k:k + 1])
                        ins.then_inc(ready, 1)
                    act.wait_ge(ready, n + 2 * j + 2)
                    act.sem_inc(free(job(j)), 1)

            n_norm = 0

            def normalise(src, t):
                nonlocal n_norm
                n_norm += 1
                act.wait_ge(rstd_ready, n_norm)
                act.activation(xn[:, t, :], src[:, t, :], ACT.Identity, bias=mv[:, t, 0:1],
                               scale=rstd[:, t, :]).then_inc(xn_ready, 1)

            def front(c, stage):
                if stage == "norm":
                    act.wait_ge(xin_loaded, 16 * (c + 1))
                    for t in range(TT):
                        normalise(xn, t)
                if stage == "lnT":
                    if c == 0:
                        act.wait_ge(mcol_ready, 1)
                    evacuate_norm(lambda j: f"lnT{j}.{c}", hT[c % 2], 0, hT_ready, KH * c)
                if stage[0] == "u":
                    q = int(stage[1])
                    name = f"u{q}.{c}"
                    if c == 0 and q == 0:
                        act.wait_ge(taps_halved, 1)
                    if c >= 2 and q == 0:
                        act.wait_ge(decay_ready, NS * (c - 1))
                    wait_job(act, name)
                    if c >= 1 and q == 1:
                        act.wait_ge(b_stored, 16 * c)
                    if 4 * c + q >= 2:
                        act.wait_ge(conv_done, 2 * (4 * c + q - 1))
                        act.wait_ge(halo_saved, 4 * c + q - 1)
                    act.activation(upre[q % 2][:, :, KW - 1:], psum(name)[:, :].rearrange("p (i t) -> p i t", i=2),
                                   ACT.Copy).then_inc(taps_ready, 1)
                    for i in range(2):
                        d = 2 * q + i
                        ins = act.activation(step[c % 2][:, d, :], psum(name)[:, i * TC:(i + 1) * TC], ACT.Identity,
                                             bias=dcols[:, CB + d:CB + d + 1],
                                             scale=dcols[:, CW + d * KW + KW - 1:CW + d * KW + KW])
                        ins.then_inc(taps_ready, 1)
                    act.wait_ge(taps_ready, 3 * (4 * c + q + 1))
                    act.sem_inc(free(name), 1)
                if stage[:4] == "tanh":
                    j = int(stage[4])
                    act.wait_ge(conv_done, 8 * c + 4 * j + 4)
                    if c >= 2:
                        wait_job(act, f"o1.{c - 2}")
                    act.activation(u[c % 2][:, 4 * j:4 * j + 4, :], step[c % 2][:, 4 * j:4 * j + 4, :],
                                   ACT.Tanh).then_inc(tanh_ready, 1)
                if stage == "xp":
                    wait_job(act, f"xp.{c}")
                    act.wait_ge(halo_saved, 4 * (c + 1))
                    act.activation(ssT[:, :], psum(f"xp.{c}")[0:XW, 0:TC], ACT.Copy).then_inc(ssT_ready, 1)
                    act.wait_ge(ssT_ready, c + 1)
                    act.sem_inc(free(f"xp.{c}"), 1)
                if stage == "dbT":
                    name = f"dbT.{c}"
                    wait_job(act, name)
                    if c >= 1:
                        act.wait_ge(b_stored, 16 * c)
                    act.activation(dtT[0:R, :], psum(name)[0:R, 0:TC], ACT.Copy).then_inc(dtT_ready, 1)
                    act.activation(bT[R:R + NS, :], psum(name)[R:R + NS, 0:TC], ACT.Copy).then_inc(bT_ready, 1)
                    act.wait_ge(dtT_ready, c + 1)
                    act.wait_ge(bT_ready, c + 1)
                    act.sem_inc(free(name), 1)
                if stage == "log":
                    act.wait_ge(u_ready, 2 * (c + 1))
                    log = step[c % 2][:, :, :].rearrange("p d t -> p (d t)")
                    for j in range(2):
                        for q in (2 * j, 2 * j + 1):
                            wait_job(act, f"dt{q}.{c}")
                            act.activation(log[:, q * 512:(q + 1) * 512], psum(f"dt{q}.{c}")[:, :],
                                           ACT.Abs).then_inc(act_chain, 1)
                        half = log[:, j * 1024:(j + 1) * 1024]
                        act.wait_ge(act_chain, 6 * c + 3 * j + 2)
                        act.activation(half, half, ACT.Exp, scale=-1.0).then_inc(act_chain, 1)
                    for j in range(2):
                        half = log[:, j * 1024:(j + 1) * 1024]
                        act.wait_ge(act_chain, 6 * c + 3 * j + 3)
                        act.activation(half, half, ACT.Ln, bias=1.0).then_inc(log_ready, 1)
                if stage == "first" and c >= 1:
                    act.wait_ge(first_ready, c)
                    act.activation(first[:], first[:], ACT.Exp).then_inc(first_exp, 1)

            def back(c, stage):
                if stage in ("g0", "g1", "g2", "g3"):
                    q = int(stage[1])
                    wait_job(act, f"g{q}.{c}")
                    if c == CHUNKS - 1:
                        if q >= 2:
                            wait_released(act, f"g{q - 2}.{c}")
                        else:
                            act.wait_ge(z_ready, 4 * c)
                    elif 4 * c + q >= 2:
                        act.wait_ge(z_ready, 4 * c + q - 1)
                    act.activation(gth[q % 2][:].rearrange("p i t -> p (i t)"), psum(f"g{q}.{c}")[:, :],
                                   ACT.Tanh, scale=0.5).then_inc(gth_ready, 1)
                if stage in ("o0", "o1", "m0", "m1"):
                    name = f"{stage}.{c}"
                    wait_job(act, name)
                    release(act.activation(xres[:, int(stage[1]), :], psum(name)[:, :], ACT.Copy), name)
                if stage in ("norm0", "norm1"):
                    for j in range(2):
                        wait_job(act, f"lnT{j}.{c + 2}" if c + 2 < CHUNKS else f"l2T{j}.{c - 1}")
                    normalise(xres, int(stage[4]))
                if stage in ("l2T0", "l2T1"):
                    t = int(stage[3])
                    if c == 0:
                        act.wait_ge(mcol_ready, 2)
                    name = f"{stage}.{c}"
                    wait_job(act, name)
                    if t == 0 and c >= 1:
                        wait_job(act, f"m1.{c - 1}")
                        wait_job(act, f"la.{c - 1}")
                    for k in range(KH):
                        act.activation(h2T[:, k, t * P:(t + 1) * P], psum(name)[:, k * P:(k + 1) * P], ACT.Identity,
                                       bias=mcol[:, 2, k:k + 1], scale=mcol[:, 3, k:k + 1]).then_inc(h2T_ready, 1)
                    act.wait_ge(h2T_ready, KH * (TT * c + t + 1))
                    act.sem_inc(free(name), 1)
                if stage == "la":
                    wait_job(act, f"la.{c}")
                    if c == 0:
                        act.wait_ge(scaled, KD + KH + 1)
                    act.activation(lt[:, TT * c:TT * c + TT, :].rearrange("p t n -> p (t n)"),
                                   psum(f"la.{c}")[:, 0:TT * P], ACT.Copy).then_inc(lt_ready, 1)
                    act.wait_ge(lt_ready, c + 1)
                    act.sem_inc(free(f"la.{c}"), 1)
                if stage == "ghT":
                    wait_job(act, f"ghT.{c}")
                    act.activation(ghT[:, :], psum(f"ghT.{c}")[0:GH, 0:TC], ACT.Copy).then_inc(ghT_ready, 1)
                    act.wait_ge(ghT_ready, c + 1)
                    act.sem_inc(free(f"ghT.{c}"), 1)

            wait_load(act, "c")
            act.activation(ccol[:, 1, :], ccol[:, 0, :], ACT.Tanh, scale=0.5).then_inc(c_tanh, 1)

            def first_sums(c):
                if c >= 1:
                    for q in range(PAIRS):
                        wait_job(act, f"y{q}.{c - 1}")
                for t in range(TT):
                    k = TT * NS * c + t
                    act.wait_ge(turned, k + 1)
                    act.wait_ge(ssn_ready, c + 1)
                    act.activation(acc[:, t, :], stT[k % 2][:], ACT.Copy,
                                   scale=ssn[c % 2][:, t, R + NS:R + NS + 1]).then_inc(added, 1)

            for c, slot in slots():
                if c == 0 and slot == 1:
                    first_sums(c)
                if slot in SCALAR_STAGES_FIRST:
                    stages(SCALAR_STAGES, c, slot, front, back)
                g = c * NS + slot + 2
                if 0 <= g < UNITS:
                    cc, n = g // NS, g % NS
                    if g == 0:
                        act.wait_ge(consts_set, 2)
                    if n == 0:
                        for q in range(PAIRS):
                            wait_released(act, f"dt{q}.{cc}")
                    if g >= N_DECAY:
                        act.wait_ge(scanned, g - N_DECAY + 1)
                    for d in range(KD):
                        ins = act.activation(decay[g % N_DECAY][:, d, 1:], step[cc % 2][:, d, 1:], ACT.Exp,
                                             scale=dcols[:, AC + n * KD + d:AC + n * KD + d + 1])
                    ins.then_inc(decay_ready, 1)
                if slot not in SCALAR_STAGES_FIRST:
                    stages(SCALAR_STAGES, c, slot, front, back)
                if 1 <= c < CHUNKS and slot == 1:
                    first_sums(c)
            act.wait_ge(diff_ready, 1)
            act.activation(ediff[:, :, 1:2], ediff[:, :, 0:1], ACT.Exp).then_inc(ediff_ready, 1)
            act.wait_ge(decay_ready, UNITS)
            for j in range(2):
                wait_job(act, f"lwT{j}")
                half = NT // 2
                act.activation(lwT[:, j * half:(j + 1) * half, :].rearrange("p t n -> p (t n)"),
                               psum(f"lwT{j}")[:, :], ACT.Copy).then_inc(lwT_ready, 1)
                act.wait_ge(lwT_ready, j + 1)
                act.sem_inc(free(f"lwT{j}"), 1)

        @block.gpsimd
        def _(pool):
            chain = Chain(pool, pool_chain)
            pool.memset(mhalf[:], -0.5)
            chain(pool.memset(halo[:], 0.0))
            chain(pool.memset(dtT[R:R + 1, :], 1.0))
            chain(pool.memset(ones[:], 1.0))
            pool.sem_inc(consts_set, 1)

            def rsqrt(dst, src, n, done):
                pool.tensor_tensor(dst, src, mhalf[:, 0:n].rearrange("p (t o) -> p t o", t=src.shape[1]),
                                   ALU.pow).then_inc(done, 1)

            n_var = 0

            def layer_rstd(t0, t1):
                nonlocal n_var
                n_var += t1 - t0
                pool.wait_ge(var_ready, 2 * n_var)
                rsqrt(rstd[:, t0:t1, :], rstd[:, t0:t1, :], t1 - t0, pool_chain)
                chain.n += 1
                pool.wait_ge(pool_chain, chain.n)
                pool.tensor_tensor(mv[:, t0:t1, 0:1], mv[:, t0:t1, 0:1], rstd[:, t0:t1, :],
                                   ALU.mult).then_inc(rstd_ready, t1 - t0)

            def front(c, stage):
                if stage == "rstd":
                    layer_rstd(0, TT)
                if stage == "rms":
                    pool.wait_ge(ms_ready, c + 1)
                    rsqrt(rinv[:], rinv[:], 3 * TT, rinv_ready)

            def back(c, stage):
                if stage[0] == "z":
                    q = int(stage[1])
                    wait_released(pool, f"g{q}.{c}")
                    wait_released(pool, f"y{q}.{c}")
                    z = u[c % 2][:, 2 * q:2 * q + 2, :].rearrange("p i t -> p (i t)")
                    pool.tensor_tensor(z, gth[q % 2][:].rearrange("p i t -> p (i t)"), z, ALU.mult).then_inc(z_ready, 1)
                if stage in ("rstd0", "rstd1"):
                    layer_rstd(int(stage[4]), int(stage[4]) + 1)
                if stage == "rgate":
                    pool.wait_ge(gvar_ready, c + 1)
                    rsqrt(rstd2[:], rstd2[:], TT, grstd_ready)

            def keep_last(g):
                chain(pool.tensor_copy(carry[:, g % NS, :].rearrange("p (d o) -> p d o", o=1),
                                       drive[g % N_DRIVE][:, :, TC - 1:TC]))

            for c, slot in slots():
                if c == 0 and 1 <= slot <= KD + KH + 1:
                    i = slot - 1
                    name, gate, w = (("wo", gar, wo[:, i, :]) if i < KD else ("wf", gbr, wf[:, i - KD, :])
                                     if i < KD + KH else ("lora", gbr, wlb[:, :]))
                    pool.wait_ge(gates_ready, 1 if i < KD else 2)
                    wait_load(pool, name)
                    pool.tensor_tensor(w, w, gate[:], ALU.mult).then_inc(scaled, 1)
                if 0 <= c < CHUNKS - 1 and slot == 14:
                    pool.wait_ge(drive_ready, NS * (c + 1) - 1)
                    for q in range(PAIRS):
                        wait_released(pool, f"dt{q}.{c + 1}")
                    pool.wait_ge(u_ready, 2 * (c + 2))
                    pool.tensor_tensor(du[:], step[(c + 1) % 2][:], u[(c + 1) % 2][:], ALU.mult).then_inc(du_ready, 1)
                    first_step = step[(c + 1) % 2][:, :, 0:1].rearrange("p d o -> p o d").broadcast_to([P, NS, KD])
                    pool.tensor_tensor(first[:], dcols[:, AC:AC + NS * KD].rearrange("p (n d) -> p n d", n=NS),
                                       first_step, ALU.mult).then_inc(first_ready, 1)
                g = c * NS + slot + 2
                if 0 <= g < UNITS:
                    j = g // NB
                    if g == 0:
                        wait_mod_done(pool)
                        for i in range(N_DECAY):
                            chain(pool.memset(decay[i][:, :, 0:1], 0.0))
                        pool.sem_inc(consts_set, 1)
                        continue
                    if g % NS == 0 or g == 1:
                        pool.wait_ge(du_ready, g // NS + 1)
                    pool.wait_ge(brep_loaded[j % N_BREP], 16 * (j // N_BREP + 1))
                    if g >= N_DRIVE:
                        pool.wait_ge(turned, TT * (g - N_DRIVE + 1))
                        if g - N_DRIVE < UNITS - NS:
                            keep_last(g - N_DRIVE)
                    bmul = pool.tensor_tensor(drive[g % N_DRIVE], du[:],
                                              brep[j % N_BREP][:, g % NB:g % NB + 1, :].broadcast_to([P, KD, TC]),
                                              ALU.mult)
                    if g < NS:
                        bmul.then_inc(drive_ready, 1)
                    else:
                        if g % NS == 0:
                            pool.wait_ge(first_exp, g // NS)
                        bmul.then_inc(pool_chain, 1)
                        kept = carry[:, g % NS, :]
                        pool.tensor_tensor(kept, first[:, g % NS, :], kept, ALU.mult).then_inc(pool_chain, 1)
                        chain.n += 2
                        pool.wait_ge(pool_chain, chain.n)
                        column = drive[g % N_DRIVE][:, :, 0:1]
                        pool.tensor_tensor(column, column, kept.rearrange("p (d o) -> p d o", o=1),
                                           ALU.add).then_inc(drive_ready, 1)
                stages(POOL_STAGES, c, slot, front, back)

        @block.vector
        def _(dve):
            chain = Chain(dve, dve_chain)
            n_stats = 0

            def norm_stats(src, t):
                nonlocal n_stats
                if n_stats >= TT:
                    dve.wait_ge(xn_ready, n_stats - TT + 1)
                chain(dve.bn_stats(stat[:, t, :], src[:, t, :]))
                chain(dve.bn_aggr(mv[:, t, :], stat[:, t, :]))
                dve.tensor_scalar(mv[:, t, 0:1], mv[:, t, 0:1], -1.0, None, ALU.mult).then_inc(var_ready, 1)
                dve.tensor_scalar(rstd[:, t, :], mv[:, t, 1:2], LN_EPS, None, ALU.add).then_inc(var_ready, 1)
                n_stats += 1

            def front(c, stage):
                if stage == "stats":
                    dve.wait_ge(xin_loaded, 16 * (c + 1))
                    for t in range(TT):
                        norm_stats(xn, t)
                    if c == 0:
                        mod_sum(0)
                        wait_load(dve, "consts")
                        dve.tensor_scalar(dcols[:, CW:DP], dcols[:, CW:DP], 0.5, None,
                                          ALU.mult).then_inc(taps_halved, 1)
                        dve.wait_ge(taps_halved, 1)
                        mod_cols(1, 0, 0)
                if stage[:4] == "conv":
                    q = int(stage[4])
                    pre = upre[q % 2]
                    x = step[c % 2]
                    tapped = {}
                    dve.wait_ge(taps_ready, 3 * (4 * c + q + 1))
                    chain(dve.tensor_copy(pre[:, :, 0:KW - 1], halo[:, 2 * q:2 * q + 2, :]))
                    for tap in range(KW - 1):
                        for i in range(2):
                            d = 2 * q + i
                            if tap:
                                dve.wait_ge(dve_chain, tapped[i])
                            ins = dve.scalar_tensor_tensor(
                                out=x[:, d, :], in0=pre[:, i, tap:tap + TC],
                                scalar=dcols[:, CW + d * KW + tap:CW + d * KW + tap + 1],
                                in1=x[:, d, :], op0=ALU.mult, op1=ALU.add)
                            if tap < KW - 2:
                                ins.then_inc(dve_chain, 1)
                                chain.n += 1
                                tapped[i] = chain.n
                            else:
                                ins.then_inc(conv_done, 1)
                    dve.tensor_copy(halo[:, 2 * q:2 * q + 2, :], pre[:, :, TC:TC + KW - 1]).then_inc(halo_saved, 1)
                if stage[:4] == "silu":
                    j = int(stage[4])
                    dve.wait_ge(tanh_ready, 2 * c + j + 1)
                    tanh = u[c % 2][:, 4 * j:4 * j + 4, :].rearrange("p d t -> p (d t)")
                    x = step[c % 2][:, 4 * j:4 * j + 4, :].rearrange("p d t -> p (d t)")
                    dve.scalar_tensor_tensor(out=tanh, in0=tanh, scalar=1.0, in1=x,
                                             op0=ALU.add, op1=ALU.mult).then_inc(u_ready, 1)
                    if c == 0 and j == 1:
                        mod_sum(1)
                if stage == "rms":
                    name = f"xpT.{c}"
                    wait_job(dve, name)
                    release(dve.tensor_copy(ss[:].rearrange("p t n -> p (t n)"), psum(name)[:, 0:TT * XW]), name)
                    wait_released(dve, name)
                    chain(dve.tensor_tensor(sq[:], ss[:], ss[:], ALU.mult))
                    dve.tensor_reduce(rinv[:, :, 0], sq[:, :, 0:R], AX_X, ALU.add)
                    chain(dve.tensor_reduce(rinv[:, :, 1:3],
                                            sq[:, :, R:].rearrange("p t (g n) -> p t g n", n=NS), AX_X, ALU.add))
                    dve.tensor_scalar(rinv[:, :, 0], rinv[:, :, 0], 1.0 / R, RMS_EPS, ALU.mult, ALU.add)
                    chain(dve.tensor_scalar(rinv[:, :, 1:3], rinv[:, :, 1:3], 1.0 / NS, RMS_EPS, ALU.mult, ALU.add))
                    dve.sem_inc(ms_ready, 1)
                if stage == "rmsn":
                    dve.wait_ge(rinv_ready, c + 1)
                    for t in range(TT):
                        for g, (a, b) in enumerate(((0, R), (R, R + NS), (R + NS, XW))):
                            ins = dve.scalar_tensor_tensor(
                                out=ssn[c % 2][:, t, a:b], in0=ss[:, t, a:b], scalar=rinv[:, t, g:g + 1],
                                in1=rows[:, R_LN + a:R_LN + b], op0=ALU.mult, op1=ALU.mult)
                    ins.then_inc(ssn_ready, 1)
                    if c == 0:
                        mod_sum(2)
                        gate_row(2, stT[0][:, 0:H], gar, 0.5)
                if stage == "delta":
                    for q in range(PAIRS):
                        dve.wait_ge(log_ready, 2 * c + q // 2 + 1)
                        x = step[c % 2][:, 2 * q:2 * q + 2, :].rearrange("p d t -> p (d t)")
                        release(dve.scalar_tensor_tensor(out=x, in0=psum(f"dt{q}.{c}")[:, :], scalar=0.0, in1=x,
                                                         op0=ALU.max, op1=ALU.add), f"dt{q}.{c}")
                    if c == 0:
                        for q in range(PAIRS):
                            pair = slice(2 * q, 2 * q + 2)
                            wait_released(dve, f"dt{q}.0")
                            ins = dve.tensor_tensor(du[:, pair, :], step[0][:, pair, :], u[0][:, pair, :], ALU.mult)
                        ins.then_inc(du_ready, 1)
                        wait_mod_done(dve)
                        dve.wait_ge(brep_loaded[0], 16)
                        dve.wait_ge(du_ready, 1)
                        dve.tensor_tensor(drive[0], du[:], brep[0][:, 0:1, :].broadcast_to([P, KD, TC]),
                                          ALU.mult).then_inc(first_drive, 1)

            def back(c, stage):
                uc = u[c % 2]
                if stage[:4] == "skip":
                    q = int(stage[4])
                    wait_job(dve, f"y{q}.{c}")
                    for i in range(2):
                        d = 2 * q + i
                        ins = dve.scalar_tensor_tensor(
                            out=uc[:, d, :], in0=uc[:, d, :], scalar=dcols[:, DP + d:DP + d + 1],
                            in1=psum(f"y{q}.{c}")[:, i * TC:(i + 1) * TC], op0=ALU.mult, op1=ALU.add)
                    release(ins, f"y{q}.{c}")
                if stage[0] == "e":
                    q = int(stage[1])
                    dve.wait_ge(gth_ready, 4 * c + q + 1)
                    release(dve.scalar_tensor_tensor(
                        out=step[(c + 1) % 2][:, 2 * q:2 * q + 2, :].rearrange("p i t -> p (i t)"),
                        in0=gth[q % 2][:].rearrange("p i t -> p (i t)"), scalar=1.0, in1=psum(f"g{q}.{c}")[:, :],
                        op0=ALU.add, op1=ALU.mult), f"g{q}.{c}")
                if stage[0] == "z" and c == CHUNKS - 1:
                    q = int(stage[1])
                    wait_released(dve, f"g{q}.{c}")
                    wait_released(dve, f"y{q}.{c}")
                    z = uc[:, 2 * q:2 * q + 2, :].rearrange("p i t -> p (i t)")
                    g2 = step[(c + 1) % 2][:, 2 * q:2 * q + 2, :].rearrange("p i t -> p (i t)")
                    dve.tensor_tensor(z, g2, z, ALU.mult).then_inc(z_ready, 1)
                elif stage[0] == "z":
                    q = int(stage[1])
                    dve.wait_ge(gth_ready, 4 * c + q + 1)
                    g2 = gth[q % 2][:].rearrange("p i t -> p (i t)")
                    release(dve.scalar_tensor_tensor(out=g2, in0=g2, scalar=1.0, in1=psum(f"g{q}.{c}")[:, :],
                                                     op0=ALU.add, op1=ALU.mult), f"g{q}.{c}")
                if stage in ("o0", "o1"):
                    t = int(stage[1])
                    name = f"o{t}.{c}"
                    wait_job(dve, name)
                    if t == 0:
                        dve.wait_ge(xres_loaded, 16 * (c + 1))
                    release(dve.tensor_tensor(xres[:, t, :], xres[:, t, :], psum(name)[:, :], ALU.add), name)
                if stage in ("st0", "st1"):
                    wait_released(dve, f"o{stage[2]}.{c}")
                    norm_stats(xres, int(stage[2]))
                if stage == "gate1":
                    name = f"gh.{c}"
                    wait_job(dve, name)
                    release(dve.tensor_tensor(gh[:], rows[:, None, R_GB1:R_GB1 + GH].broadcast_to([P, TT, GH]),
                                              psum(name)[:, 0:TT * GH].rearrange("p (t n) -> p t n", t=TT),
                                              ALU.add), name)
                    wait_released(dve, name)
                    for t in range(TT):
                        ins = dve.bn_stats(stat2[:, t, :], gh[:, t, :])
                    chain(ins)
                    for t in range(TT):
                        ins = dve.bn_aggr(mv2[:, t, :], stat2[:, t, :])
                    chain(ins)
                    dve.tensor_scalar(rstd2[:], mv2[:, :, 1:2], LN_EPS, None, ALU.add).then_inc(gvar_ready, 1)
                if stage == "gate2":
                    dve.wait_ge(grstd_ready, c + 1)
                    for t in range(TT):
                        ins = dve.tensor_scalar(gh[:, t, :], gh[:, t, :], mv2[:, t, 0:1], rstd2[:, t, :],
                                                ALU.subtract, ALU.mult)
                    chain(ins)
                    chain(dve.tensor_tensor(gh[:], gh[:], rows[:, None, R_GAM:R_GAM + GH].broadcast_to([P, TT, GH]),
                                            ALU.mult))
                    chain(dve.tensor_tensor(gh[:], gh[:], rows[:, None, R_BET:R_BET + GH].broadcast_to([P, TT, GH]),
                                            ALU.add))
                    dve.tensor_scalar(gh[:], gh[:], 0.0, None, ALU.max).then_inc(gh_ready, 1)
                if stage in ("m0", "m1"):
                    t = int(stage[1])
                    name = f"m{t}.{c}"
                    wait_job(dve, name)
                    release(dve.tensor_tensor(xres[:, t, :], xres[:, t, :], psum(name)[:, :], ALU.add), name)
                if stage == "top":
                    name = f"gt.{c}"
                    wait_job(dve, name)
                    release(dve.tensor_tensor(gates[:], rows[:, None, R_GB2:R_GB2 + NE].broadcast_to([P, TT, NE]),
                                              psum(name)[:, 0:TT * NE].rearrange("p (t n) -> p t n", t=TT),
                                              ALU.add), name)
                    wait_released(dve, name)
                    for t in range(TT):
                        ins = dve.max(topv[:, TT * c + t, :], gates[:, t, :])
                    chain(ins)
                    for t in range(TT):
                        ins = dve.max_index(topi[:, TT * c + t, :], topv[:, TT * c + t, :], gates[:, t, :])
                    chain(ins)

            def scan(g):
                dve.wait_ge(decay_ready, g + 1)
                if g == 0:
                    dve.wait_ge(first_drive, 1)
                else:
                    dve.wait_ge(drive_ready, g)
                v = drive[g % N_DRIVE]
                flat = v.rearrange("p d t -> p (d t)")
                dve.tensor_tensor_scan(flat, decay[g % N_DECAY].rearrange("p d t -> p (d t)"), flat, 0.0,
                                       ALU.mult, ALU.add).then_inc(scanned, 1)

            def add_states(g):
                c, n = g // NS, g % NS
                for t in range(TT):
                    k = TT * g + t
                    if n > 0:
                        dve.wait_ge(turned, k + 1)
                    cn = ssn[c % 2][:, t, R + NS + n:R + NS + n + 1]
                    if n > 0:
                        dve.wait_ge(added, k - (t == 1 or n > 1))
                        dve.scalar_tensor_tensor(out=acc[:, t, :], in0=stT[k % 2][:], scalar=cn, in1=acc[:, t, :],
                                                 op0=ALU.mult, op1=ALU.add).then_inc(added, 1)

            def mod_sum(i):
                w = wmod[:, :, i * 1024:(i + 1) * 1024]
                for k in range(KH):
                    if i > 0 and k == 0:
                        wait_load(dve, f"wm{i}")
                    if i == 0 and k % 2 == 0:
                        wait_load(dve, f"wm0{'ab'[k // 2]}")
                    ck = ccol[:, 2, k:k + 1]
                    if k == 0:
                        chain(dve.tensor_scalar(w[:, 0, :], w[:, 0, :], ck, None, ALU.mult))
                    elif k < KH - 1:
                        chain(dve.scalar_tensor_tensor(out=w[:, 0, :], in0=w[:, k, :], scalar=ck, in1=w[:, 0, :],
                                                       op0=ALU.mult, op1=ALU.add))
                    else:
                        dve.scalar_tensor_tensor(out=w[:, 0, :], in0=w[:, k, :], scalar=ck, in1=w[:, 0, :],
                                                 op0=ALU.mult, op1=ALU.add).then_inc(mod_summed, 1)

            def gate_row(ready, ps, dst, factor):
                dve.wait_ge(mod_ready, ready)
                dve.tensor_scalar(dst[:], ps, 0.0, 2.0 * factor, ALU.is_ge, ALU.mult)
                chain(dve.tensor_scalar(tmp, ps, -1.0, None, ALU.mult))
                chain(dve.scalar_tensor_tensor(out=tmp, in0=ps, scalar=0.25, in1=tmp, op0=ALU.max, op1=ALU.max))
                chain(dve.scalar_tensor_tensor(out=dst[:], in0=dst[:], scalar=-factor, in1=tmp,
                                               op0=ALU.add, op1=ALU.mult))
                dve.sem_inc(gates_ready, 1)

            def mod_cols(ready, at, i):
                dve.wait_ge(mod_ready, ready)
                dve.tensor_copy(mcol[:, i, :], stT[1][:, at:at + KH])
                chain(dve.tensor_scalar(mcol[:, i + 1, :], stT[1][:, at + KH:at + 2 * KH], 1.0, None, ALU.add))
                dve.sem_inc(mcol_ready, 1)

            wait_load(dve, "c")
            chain(dve.tensor_scalar(ccol[:, 2, :], ccol[:, 0, :], 0.5, None, ALU.mult))
            dve.wait_ge(c_tanh, 1)
            chain(dve.scalar_tensor_tensor(out=ccol[:, 2, :], in0=ccol[:, 1, :], scalar=1.0, in1=ccol[:, 2, :],
                                           op0=ALU.add, op1=ALU.mult))
            dve.wait_ge(consts_set, 1)
            for c, slot in slots():
                g = c * NS + slot
                if 0 <= g < UNITS:
                    scan(g)
                if g == 0:
                    mod_cols(3, 2 * KH, 2)
                    gate_row(4, stT[1][:, H:2 * H], gbr, 1.0)
                if slot in VECTOR_STAGES_FIRST:
                    stages(VECTOR_STAGES, c, slot, front, back)
                if 0 < g <= UNITS:
                    add_states(g - 1)
                if slot not in VECTOR_STAGES_FIRST:
                    stages(VECTOR_STAGES, c, slot, front, back)
            chain(dve.tensor_copy(idx[:], topi[:, :, 0:TOPK]))
            dve.tensor_tensor(hot[:].rearrange("p t k e -> p (t k) e"),
                              idx[:].rearrange("p t (k o) -> p (t k) o", o=1).broadcast_to([P, NT * TOPK, NE]),
                              iota[:, None, :].broadcast_to([P, NT * TOPK, NE]), ALU.is_equal).then_inc(hot_ready, 1)
            dve.tensor_tensor(ediff[:, :, 0:1], topv[:, :, 1:2], topv[:, :, 0:1], ALU.subtract).then_inc(diff_ready, 1)
            dve.wait_ge(ediff_ready, 1)
            chain(dve.tensor_scalar(prob[:, :, 0:1], ediff[:, :, 1:2], 1.0, None, ALU.add))
            chain(dve.reciprocal(prob[:, :, 0:1], prob[:, :, 0:1]))
            chain(dve.tensor_tensor(prob[:, :, 1:2], prob[:, :, 0:1], ediff[:, :, 1:2], ALU.mult))
            dve.wait_ge(hot_ready, 1)
            chain(dve.tensor_tensor(hotw.rearrange("p t k e -> p (t k) e"),
                                    hot[:].rearrange("p t k e -> p (t k) e"),
                                    prob[:].rearrange("p t (k o) -> p (t k) o", o=1).broadcast_to([P, NT * TOPK, NE]),
                                    ALU.mult))
            back(CHUNKS - 1, "m0")
            wait_job(dve, f"count.{CHUNKS - 1}")
            count = f"count.{CHUNKS - 1}"
            allowed_ke = allowed[:].rearrange("p k e -> p (k e)")
            release(dve.tensor_scalar(allowed_ke, psum(count)[:, 0:TOPK * NE], float(CAP), None, ALU.is_le), count)
            wait_released(dve, count)
            chain(dve.tensor_tensor(hotw.rearrange("p t k e -> p t (k e)"),
                                    hotw.rearrange("p t k e -> p t (k e)"),
                                    allowed_ke[:, None, :].broadcast_to([P, NT, TOPK * NE]), ALU.mult))
            chain(dve.tensor_tensor(wexp, hotw[:, :, 0, :], hotw[:, :, 1, :], ALU.add))
            dve.wait_ge(lt_ready, CHUNKS)
            dve.scalar_tensor_tensor(
                out=lw.rearrange("p t (e r) -> p (t e) r", e=NE),
                in0=lt[:].rearrange("p t (e r) -> p (t e) r", e=NE), scalar=ALPHA,
                in1=wexp.rearrange("p t (e o) -> p (t e) o", o=1).broadcast_to([P, NT * NE, ER]),
                op0=ALU.mult, op1=ALU.mult).then_inc(lw_ready, 1)
            back(CHUNKS - 1, "m1")
            dve.wait_ge(x2_back, 16)
            for t in range(NT):
                name = f"lo{t}"
                wait_job(dve, name)
                if t >= 4:
                    dve.wait_ge(out_stored[t % 4], 16 * (t // 4))
                x2 = x2r[:, t, :] if t < NT - TT else xres[:, t - (NT - TT), :]
                release(dve.tensor_tensor(fin[:, t % 4, :], x2, psum(name)[:, :], ALU.add), name)


def kernel(**inputs):
    import numpy as np
    import concourse.bacc as bacc
    from concourse.bass_utils import run_bass_kernel_spmd

    a = {k: np.asarray(v) for k, v in inputs.items()}

    def tiles(m):
        return np.ascontiguousarray(m.reshape(-1, P, m.shape[1]).transpose(1, 0, 2))

    def cols(v):
        return v.reshape(KD, P, -1).transpose(1, 0, 2).reshape(P, -1)

    w_in = a["L0_attn_W_in"].T
    a_cols = a["L0_attn_A"].reshape(KD, P, NS).transpose(1, 2, 0).reshape(P, -1)
    arrays = {
        "x": a["L0_attn_hidden_states"].reshape(T, H),
        "w_in_u": tiles(w_in[:, :D]),
        "w_in_g": tiles(w_in[:, D:]),
        "dcols": np.concatenate([cols(a["L0_attn_conv_w"]), cols(a["L0_attn_conv_b"]),
                                 cols(a["L0_attn_D_param"]), a_cols], axis=1),
        "w_x": tiles(a["L0_attn_Wx"].T),
        "w_dt": np.concatenate([a["L0_attn_Wdt"].T, a["L0_attn_dt_bias"][None, :]], axis=0),
        "w_out": tiles(a["L0_attn_W_out"].T),
        "w_ffn": tiles(a["L0_ffn_weight"].T),
        "lora_a": tiles(a["L0_ffn_lora_A"].transpose(1, 0, 2).reshape(H, NE * ER)),
        "lora_b": a["L0_ffn_lora_B"].reshape(NE * ER, H),
        "gw1": tiles(a["L0_ffn_gw1"].T),
        "gw2": a["L0_ffn_gw2"].T,
        "rows": np.concatenate([a["L0_attn_dt_ln_w"], a["L0_attn_b_ln_w"], a["L0_attn_c_ln_w"], a["L0_ffn_gb1"],
                                a["L0_ffn_ln_gamma"], a["L0_ffn_ln_beta"], a["L0_ffn_gb2"]])[None, :],
        "c": a["L0_c"].reshape(KH, P).T,
        "w_mod": tiles(a["L0_wmod"]),
        "ident": np.eye(P, dtype=np.float32),
        "iota": np.tile(np.arange(NE, dtype=np.float32), (P, 1)),
    }
    nc = bacc.Bacc("TRN2", target_bir_lowering=False, num_devices=1)
    named, args = {}, []
    for name, v in arrays.items():
        v = np.ascontiguousarray(v)
        named[f"in_{name}"] = v
        args.append(nc.dram_tensor(f"in_{name}", v.shape, mybir.dt.from_np(v.dtype), kind="ExternalInput").ap())
    args.append(nc.dram_tensor("out", (T, H), F32, kind="ExternalOutput").ap())
    adaln_block(nc, *args)
    r = run_bass_kernel_spmd(nc, [named], core_ids=[0])
    return r.results[0]["out"].reshape(1, T, H)
```
